# Optimizing a Trainium2 kernel written in Bass

```python
import numpy as np
import jax
import jax.numpy as jnp

def _softmax(x, axis=-1):
    return jax.nn.softmax(x, axis=axis)

def _gelu(x):
    return jax.nn.gelu(x, approximate=True)

def _silu(x):
    return jax.nn.silu(x)

def _sigmoid(x):
    return jax.nn.sigmoid(x)

def _layernorm(x, axis=-1, eps=1e-05):
    m = jnp.mean(x, axis=axis, keepdims=True)
    v = jnp.var(x, axis=axis, keepdims=True)
    return (x - m) / jnp.sqrt(v + eps)

def _scatter_add(tgt, idx, src, axis=0):
    return tgt.at[idx].add(src)

def _segment_sum(src, seg, n):
    return jax.ops.segment_sum(src, seg, n)
kernel_name = 'mk_flamingo_gated_d1_seqx_r2_bcf1f4'

def setup_inputs(seed: int=0):
    np.random.seed(seed)
    _w = jnp.asarray

    def _rec_inputs():
        import jax
        import jax.numpy as jnp
        _rk = jax.random.key(seed)
        x = -0.000125 + 0.9999 * jax.random.normal(jax.random.fold_in(_rk, 1), (2, 1024, 2048), jnp.float32)
        _lenS = 1024 - jax.random.randint(jax.random.fold_in(_rk, 7), (2,), 0, max(1, 1024 // 4) + 1, jnp.int32)
        _lenS2 = 2048 - jax.random.randint(jax.random.fold_in(_rk, 8), (2,), 0, max(1, 2048 // 4) + 1, jnp.int32)
        _ctx_4096P = jax.random.normal(jax.random.fold_in(_rk, 11), (2, 16, 2048), jnp.float32)
        _ctx_4096c = jax.random.dirichlet(jax.random.fold_in(_rk, 511), 0.3 * jnp.ones((16,), jnp.float32), (2, 2048))
        _ctx_4096t = jnp.einsum('bsk,bkd->bsd', _ctx_4096c, _ctx_4096P)
        _ctx_4096t = _ctx_4096t * jax.lax.rsqrt(jnp.mean(jnp.square(_ctx_4096t)) + 1e-12) * 0.953939
        ctx_4096 = -5.72187e-05 + 0.999849 * (_ctx_4096t + 0.3 * jax.random.normal(jax.random.fold_in(_rk, 611), (2, 2048, 2048), jnp.float32))
        _g = jax.random.normal(jax.random.fold_in(_rk, 9001), (2, 1), jnp.float32)
        _g = jnp.sign(_g) * jnp.maximum(jnp.abs(_g), 1.0) + (_g == 0) * 1.0
        g_xattn = _g[0]
        g_ffn = _g[1]
        return (x, ctx_4096, g_xattn, g_ffn)
    x, ctx_4096, g_xattn, g_ffn = _rec_inputs()

    def _L0_xattn_setup():
        import jax, jax.numpy as jnp
        import numpy as np
        QMIN = 0.0
        QMAX = 255.0

        def fake_quant(x, scale, zp):
            s = scale.reshape(())
            z = zp.reshape(())
            q = jnp.clip(jnp.round(x / s + z), QMIN, QMAX)
            return (q - z) * s
        key = jax.random.key(seed)
        k1, k2 = jax.random.split(key)
        B, M, K, N = (4, 1024, 2048, 2048)
        x1 = jax.random.normal(k1, (B, M, K), dtype=jnp.float32)
        x2 = jax.random.normal(k2, (B, K, N), dtype=jnp.float32)
        x1_scale = jnp.full((1,), 8.0 / 255.0, dtype=jnp.float32)
        x1_zp = jnp.full((1,), 128.0, dtype=jnp.float32)
        x2_scale = jnp.full((1,), 8.0 / 255.0, dtype=jnp.float32)
        x2_zp = jnp.full((1,), 128.0, dtype=jnp.float32)
        return {'x1': x1, 'x2': x2, 'x1_scale': x1_scale, 'x1_zp': x1_zp, 'x2_scale': x2_scale, 'x2_zp': x2_zp}
    _L0_xattn_all = _L0_xattn_setup()
    _L0_xattn_in = {k: v for k, v in _L0_xattn_all.items() if k in ('x1_scale', 'x1_zp', 'x2_scale', 'x2_zp')}
    del _L0_xattn_all

    def _L0_ffn_setup():
        import jax, jax.numpy as jnp
        import numpy as np
        R = 16
        ALPHA = 32
        SCALING = ALPHA / R
        E = 8
        TOP_K = 2
        key = jax.random.key(seed)
        ks = jax.random.split(key, 5)
        B, S, D = (4, 1024, 2048)
        x = jax.random.normal(ks[0], (B, S, D), dtype=jnp.float32)
        base_W = jax.random.normal(ks[1], (D, D), dtype=jnp.float32) * 0.02
        router_W = jax.random.normal(ks[2], (E, D), dtype=jnp.float32) * 0.02
        lora_A = jax.random.normal(ks[3], (E, D, R), dtype=jnp.float32) * 0.02
        lora_B = jax.random.normal(ks[4], (E, R, D), dtype=jnp.float32) * 0.02
        return {'x': x, 'base_W': base_W, 'router_W': router_W, 'lora_A': lora_A, 'lora_B': lora_B}
    _L0_ffn_all = _L0_ffn_setup()
    _L0_ffn_in = {k: v for k, v in _L0_ffn_all.items() if k in ('base_W', 'router_W', 'lora_A', 'lora_B')}
    del _L0_ffn_all
    return {'x': x, 'ctx_4096': ctx_4096, 'g_xattn': g_xattn, 'g_ffn': g_ffn, 'L0_xattn_x1_scale': _L0_xattn_in['x1_scale'], 'L0_xattn_x1_zp': _L0_xattn_in['x1_zp'], 'L0_xattn_x2_scale': _L0_xattn_in['x2_scale'], 'L0_xattn_x2_zp': _L0_xattn_in['x2_zp'], 'L0_ffn_base_W': _L0_ffn_in['base_W'], 'L0_ffn_router_W': _L0_ffn_in['router_W'], 'L0_ffn_lora_A': _L0_ffn_in['lora_A'], 'L0_ffn_lora_B': _L0_ffn_in['lora_B']}

def reference(x, ctx_4096, g_xattn, g_ffn, L0_xattn_x1_scale, L0_xattn_x1_zp, L0_xattn_x2_scale, L0_xattn_x2_zp, L0_ffn_base_W, L0_ffn_router_W, L0_ffn_lora_A, L0_ffn_lora_B):
    import jax
    import jax.numpy as jnp

    def _L0_xattn_ref(x1, x2, x1_scale, x1_zp, x2_scale, x2_zp):
        import jax, jax.numpy as jnp
        import numpy as np
        QMIN = 0.0
        QMAX = 255.0

        def fake_quant(x, scale, zp):
            s = scale.reshape(())
            z = zp.reshape(())
            q = jnp.clip(jnp.round(x / s + z), QMIN, QMAX)
            return (q - z) * s
        q1 = fake_quant(x1, x1_scale, x1_zp)
        q2 = fake_quant(x2, x2_scale, x2_zp)
        return jnp.matmul(q1, q2)

    def _L0_ffn_ref(x, base_W, router_W, lora_A, lora_B):
        import jax, jax.numpy as jnp
        import numpy as np
        R = 16
        ALPHA = 32
        SCALING = ALPHA / R
        E = 8
        TOP_K = 2
        base = jnp.einsum('bsd,od->bso', x, base_W)
        logits = jnp.einsum('bsd,ed->bse', x, router_W)
        probs = jax.nn.softmax(logits.astype(jnp.float32), axis=-1)
        top_vals, top_idx = jax.lax.top_k(probs, TOP_K)
        rw = top_vals / jnp.sum(top_vals, axis=-1, keepdims=True)
        w_dense = jnp.sum(jax.nn.one_hot(top_idx, E, dtype=rw.dtype) * rw[..., None], axis=-2).astype(x.dtype)
        mid = jnp.einsum('bsd,edr->bser', x, lora_A)
        mid = mid * w_dense[..., None]
        inc = jnp.einsum('bser,erd->bsd', mid, lora_B)
        return base + inc * SCALING
    x = x + jnp.tanh(g_xattn[0]) * _L0_xattn_ref(_layernorm(x, axis=-1), ctx_4096, L0_xattn_x1_scale, L0_xattn_x1_zp, L0_xattn_x2_scale, L0_xattn_x2_zp)
    x = x + jnp.tanh(g_ffn[0]) * _L0_ffn_ref(_layernorm(x, axis=-1), L0_ffn_base_W, L0_ffn_router_W, L0_ffn_lora_A, L0_ffn_lora_B)
    return x

_drawn_inputs = setup_inputs


def setup_inputs(seed=0):
    import zlib

    import numpy as np

    out = dict(_drawn_inputs(seed))
    spreads = {}
    factors = {'L0_ffn_router_W': 8.0, 'L0_ffn_lora_A': 8.0, 'L0_ffn_lora_B': 8.0}
    for name, (base, spread) in spreads.items():
        noise = np.random.default_rng([zlib.crc32(name.encode()), seed]).standard_normal(out[name].shape)
        drawn = base * np.exp(spread * noise) if base else spread * noise
        out[name] = jnp.asarray(drawn.astype(out[name].dtype))
    for name, factor in factors.items():
        out[name] = (out[name] * factor).astype(out[name].dtype)
    return out
```

```python
import concourse.bass as bass
from concourse import mybir
from contextlib import ExitStack

F32 = mybir.dt.float32
F32R = mybir.dt.float32r
BF16 = mybir.dt.bfloat16
F16 = mybir.dt.float16
U8 = mybir.dt.uint8
ALU = mybir.AluOpType
ACT = mybir.ActivationFunctionType
AX = mybir.AxisListType

P = 128
D = 2048
TOK = 2048
K = D // P
NW = 512
NB = D // NW
GT = 512
G = TOK // GT
M = GT // P
TILES = G * M
ITS = G * NB
E, R = 8, 16
ER = E * R
AR = ER + E
TOP_K = 2
SCALING = 2.0
EPS = 1e-5
MID = 128.0
PK = 4
CP = K // PK
CTX_STEP = {0: 1, 1: 2, 2: 3, 5: 4, 6: 5, 7: 6, 8: 7}
WK = 2
WP = K // WK
WG = NB * WP
RING = 4
LEAD = 2 * RING
CHAIN_B = 50
KIB = 1024


class Chain:

    def __init__(self, eng, sem, base=0):
        self.eng, self.sem, self.base, self.n = eng, sem, base, 0

    def __call__(self, ins):
        self.n += 1
        ins.then_inc(self.sem, 1)
        self.eng.wait_ge(self.sem, self.base + self.n)


def build(nc, x, ctx, wt, ar, lb, scal, x1s, out):
    es = ExitStack()
    with es:
        top = nc.sbuf_base

        def at(name, off, shape, dt):
            return nc.alloc_sbuf_tensor_at(name, shape, dt, offset=off)

        def psum(name, shape, dt):
            return es.enter_context(nc.psum_tensor(name, shape, dt))

        def sem(name):
            return es.enter_context(nc.semaphore(name))

        XG0 = (top + 31) // 32 * 32
        XG1 = XG0 + 32 * KIB
        AT0 = XG1 + 32 * KIB
        AT1 = AT0 + 16 * KIB
        CTX = AT1 + 16 * KIB
        CST = CTX + 64 * KIB
        SMALL = CST + 20 * KIB
        LAST = SMALL + 21 * KIB
        xg = [at("x_group_even", XG0, [P, M, D], F32), at("x_group_odd", XG1, [P, M, D], F32)]
        aT = [at("aT_even", AT0, [P, K, GT], BF16), at("aT_odd", AT1, [P, K, GT], BF16)]
        ctxq = at("ctx_quant", CTX, [P, NB, K, NW], BF16)
        cst = [at(f"ctx_stage{s}", CST + 8 * KIB * s, [P, PK, NW], F32) for s in range(2)]
        cu8 = [at(f"ctx_u8_{s}", CST + 16 * KIB + 2 * KIB * s, [P, PK, NW], U8) for s in range(2)]
        anat = at("a_rows", SMALL, [P, D], BF16)
        xu8 = at("x_u8", SMALL + 4 * KIB, [P, D], U8)
        csum = at("ctx_part_sums", SMALL + 6 * KIB, [P, NB, NW], F16)
        half = at("ctx_half_sums", SMALL + 10 * KIB, [P, 2, NW], F16)
        quart = at("ctx_quarter_sums", SMALL + 12 * KIB, [P, NW], F16)
        colb = [at(f"col_term{s}", SMALL + 13 * KIB + 2 * KIB * s, [P, NW], F32) for s in range(2)]
        yev = [at(f"y_evac{s}", SMALL + 17 * KIB + 2 * KIB * s, [P, NW], F32) for s in range(2)]
        wst = [at(f"w_stage{s}", AT0 + 4 * KIB * s, [P, WK * NW], F32) for s in range(RING)]
        wh = [at(f"w_hi{s}", XG1 + 8 * KIB * s, [P, WK * NW], F32R) for s in range(RING)]
        wl = [at(f"w_lo{s}", XG1 + 8 * KIB * s + 4 * KIB, [P, WK * NW], F32R) for s in range(RING)]
        hh = at("hT_hi", CTX, [P, K, GT], F32R)
        hl = at("hT_lo", CTX + 32 * KIB, [P, K, GT], F32R)
        arh = at("ar_hi", CST, [P, K, AR], F32R)
        arl = at("ar_lo", CST + 9 * KIB, [P, K, AR], F32R)
        bh = at("b_hi", AT1, [P, D], F32R)
        bl = at("b_lo", AT1 + 8 * KIB, [P, D], F32R)
        res = [at(f"residual{m}", SMALL + 2 * KIB * m, [P, NW], F32) for m in range(M)]
        mids = at("mid_scaled", SMALL + 8 * KIB, [P, M, E, R], F32)
        mth = at("midT_hi", SMALL + 10 * KIB, [P, GT], F32R)
        mtl = at("midT_lo", SMALL + 12 * KIB, [P, GT], F32R)
        mid = at("mid", SMALL + 14 * KIB, [P, M, AR], F32)
        rank = at("router_rank", SMALL + 17 * KIB, [P, M, E, E], F32)
        rankeq = at("router_rank_eq", SMALL + 18 * KIB, [P, M, E, E], F32)
        o = [LAST]

        def keep(name, shape, dt, size):
            off, o[0] = o[0], o[0] + (size + 31) // 32 * 32
            return at(name, off, shape, dt)

        idf = keep("identity_f32", [P, P], F32, 512)
        idb = keep("identity_bf16", [P, P], BF16, 256)
        ones = keep("ones_f16", [P, P], F16, 256)
        tri = keep("earlier_expert", [P, E, E], F32, 256)
        sc = keep("scalars", [P, 6], F32, 24)
        th = keep("gates", [P, 2], F32, 8)
        cst_ = keep("constants", [P, 8], F32, 32)
        st = keep("bn_chunks", [P, 4 * 6], F32, 96)
        st2 = keep("bn_chunks_group", [P, M, 4 * 6], F32, 384)
        mv = keep("mean_var", [P, M, 2], F32, 32)
        ve = keep("var_eps", [P, M], F32, 16)
        sd = keep("std", [P, M], F32, 16)
        rs = keep("rstd", [P, M], F32, 16)
        nt = keep("newton", [P, M], F32, 16)
        qs = keep("quant_scale_bias", [P, 4], F32, 16)
        asum = keep("a_row_sum", [P, 1], F32, 4)
        crow = keep("row_terms", [P, TILES], F32, 64)
        lg = keep("logits_minus_max", [P, M, E], F32, 128)
        ex = keep("exp_logits", [P, M, E], F32, 128)
        rk = keep("rank", [P, M, E], F32, 128)
        wsel = keep("expert_weights", [P, M, E], F32, 128)
        mx = keep("logit_max", [P, M], F32, 16)
        den = keep("weight_sum", [P, M], F32, 16)
        assert o[0] <= nc.sbuf_usable_end, (o[0], nc.sbuf_usable_end)

        s1, z1, s2, z2 = (sc[:, i:i + 1] for i in range(4))
        inv1, inv2, cg, d1, d2, cd1, cd2, ckd = (cst_[:, i:i + 1] for i in range(8))
        gate2 = th[:, 1:2]

        acc = [psum(f"acc{m}", [P, NW], F32) for m in range(M)]
        tpa = psum("aT_psum", [P, K, P], BF16)
        tpb = [tpa[:, 8 * s:8 * s + 8, :].rearrange("p a b -> p (a b)").bitcast(F32) for s in range(2)]
        colp = psum("col_psum", [P, NW], F32)

        s_const = sem("s_const")
        s_gate = sem("s_gate")
        s_cst = sem("s_cst")
        s_id = sem("s_id")
        s_chain = sem("s_chain")
        x_in = [[sem(f"x_in{a}{m}") for m in range(M)] for a in range(2)]
        var_ready = sem("var_ready")
        std_ready = sem("std_ready")
        qs_ready = sem("qs_ready")
        xu8_ready = sem("xu8_ready")
        a_ready = sem("a_ready")
        tp_ready = sem("tp_ready")
        aT_ready = sem("aT_ready")
        c_in = [sem(f"c_in{s}") for s in range(2)]
        cu8_ready = sem("cu8_ready")
        c_conv = sem("c_conv")
        block_ready = sem("block_ready")
        col_ready = sem("col_ready")
        colb_ready = sem("colb_ready")
        pool_add = sem("pool_add")
        pe_unit = sem("pe_unit")
        evac_done = sem("evac_done")
        x1_ready = sem("x1_ready")
        x1_stored = [sem(f"x1_stored{a}") for a in range(2)]
        s_chain_b = sem("s_chain_b")
        g_in = [sem(f"g_in{m}") for m in range(M)]
        xn_ready = sem("xn_ready")
        var2_ready = sem("var2_ready")
        std2_ready = sem("std2_ready")
        w_in = [sem(f"w_in{s}") for s in range(RING)]
        wh_ready = sem("wh_ready")
        wl_ready = sem("wl_ready")
        w_used = sem("w_used")
        t_ready = sem("t_ready")
        hh_ready = sem("hh_ready")
        hl_ready = sem("hl_ready")
        ar_done = sem("ar_done")
        ar_evac = sem("ar_evac")
        lg_ready = sem("lg_ready")
        ex_ready = sem("ex_ready")
        mids_ready = sem("mids_ready")
        mt_ready = sem("mt_ready")
        mth_ready = sem("mth_ready")
        mtl_ready = sem("mtl_ready")
        acc_done = sem("acc_done")
        r_in = [sem(f"r_in{m}") for m in range(M)]
        out_ready = sem("out_ready")
        out_stored = [sem(f"out_stored{m}") for m in range(M)]

        def rows(t, g, m, n):
            return t[bass.ds(g * GT + m * P, P), n * NW:(n + 1) * NW]

        def w_piece(X):
            Y = X % WG
            k0, n = WK * (Y % WP), Y // WP
            return wt[k0 * P:(k0 + WK) * P, n * NW:(n + 1) * NW].rearrange("(k p) n -> p k n", p=P)

        def lead_piece(i):
            return 4 * AR if i < RING else NW

        block = es.enter_context(nc.Block())

        @block.sync
        def _(sp):
            def load_x(t):
                g, m = t // M, t % M
                if g >= 2:
                    sp.wait_ge(x1_stored[g % 2], 16 * NB * (g // 2))
                sp.dma_start(xg[g % 2][:, m, :], x[t * P:(t + 1) * P, :]).then_inc(x_in[g % 2][m], 16)

            def load_ctx(q):
                c, p = q // CP, q % CP
                b, n = c // NB, c % NB
                if q >= 2:
                    sp.wait_ge(cu8_ready, q - 1)
                src = ctx[b, p * PK * P:(p + 1) * PK * P, n * NW:(n + 1) * NW]
                sp.dma_start(cst[q % 2][:, :, :], src.rearrange("(k p) n -> p k n", p=P))\
                    .then_inc(c_in[q % 2], 16)

            def load_group(g):
                for m in range(M):
                    sp.dma_start(xg[0][:, m, :], x1s[bass.ds(g * GT + m * P, P), :])\
                        .then_inc(g_in[m], 16)

            def load_lead(i, slot):
                w = lead_piece(i)
                if i < RING:
                    src = ar[4 * i * P:4 * (i + 1) * P, :].rearrange("(k p) n -> p k n", p=P)
                    dst = wst[slot][:, 0:w].rearrange("p (k n) -> p k n", n=AR)
                else:
                    src, dst = lb[:, (i - RING) * NW:(i - RING + 1) * NW], wst[slot][:, 0:w]
                sp.dma_start(dst, src).then_inc(w_in[slot], 16)

            def load_w(X):
                sp.dma_start(wst[X % RING][:, :].rearrange("p (k n) -> p k n", n=NW), w_piece(X))\
                    .then_inc(w_in[X % RING], 16)

            def load_res(g, n):
                for m in range(M):
                    sp.dma_start(res[m][:, :], rows(x1s, g, m, n)).then_inc(r_in[m], 16)

            sp.dma_start(sc[:, :], scal).then_inc(s_const, 16)
            load_x(0)
            for p in range(CP):
                load_ctx(p)
                if p + 1 < M:
                    load_x(p + 1)
            load_x(M)
            for i in range(ITS):
                c = CTX_STEP.get(i)
                if c is not None:
                    for p in range(CP):
                        load_ctx(CP * c + p)
                if M + 1 + i < TILES:
                    load_x(M + 1 + i)
                if i == ITS - NB:
                    sp.wait_ge(x1_stored[0], 16 * NB * 2)
                    load_group(0)
                    sp.wait_ge(pe_unit, M * NB * (G - 1))
                    for r in range(RING):
                        load_lead(r, r)
            for a in range(2):
                sp.wait_ge(x1_stored[a], 16 * NB * 2)
            for X in range(RING):
                sp.wait_ge(wl_ready, X + 1)
                load_w(X)
            load_res(0, 0)
            for r in range(RING):
                sp.wait_ge(wl_ready, RING + r + 1)
                load_lead(RING + r, r)

            def group(g, last):
                for j in range(NB):
                    for q in range(WP):
                        X = WP * j + RING + q
                        if not (last and X >= WG):
                            sp.wait_ge(wl_ready, g * WG + (LEAD + X - RING + 1))
                            load_w(X)
                        if j == 0 and q == 0 and not last:
                            sp.wait_ge(t_ready, g * K + K)
                            load_group(g + 1)
                    if not (last and j == NB - 1):
                        for m in range(M):
                            sp.wait_ge(out_stored[m], g * (16 * NB) + 16 * (j + 1))
                        if j < NB - 1:
                            load_res(g, j + 1)
                        else:
                            load_res(g + 1, 0)

            with sp.Fori(0, G - 1) as g:
                group(g, False)
            group(G - 1, True)
            for m in range(M):
                sp.wait_ge(out_stored[m], 16 * ITS)

        @block.gpsimd
        def _(pool):
            pool.memset(idf[:, :], 0.0).then_inc(s_id, 1)
            pool.memset(idb[:, :], 0.0).then_inc(s_id, 1)
            pool.memset(ones[:, :], 1.0).then_inc(s_id, 1)
            pool.memset(tri[:, :, :], 1.0).then_inc(s_id, 1)
            pool.wait_ge(s_id, 4)
            for t in (idf, idb):
                pool.affine_select(out=t[:, :], in_=t[:, :], compare_op=ALU.not_equal, fill=1.0, base=0,
                                   pattern=[[-1, P]], channel_multiplier=1).then_inc(s_id, 1)
            pool.affine_select(out=tri[:, :, :], in_=tri[:, :, :], compare_op=ALU.is_gt, fill=0.0, base=0,
                               pattern=[[1, E], [-1, E]], channel_multiplier=0).then_inc(s_id, 1)
            for i in range(ITS):
                g, n = i // NB, i % NB
                pool.wait_ge(colb_ready, i + 1)
                for m in range(M):
                    pool.wait_ge(xu8_ready, M * g + m + 1)
                    blk = xg[g % 2][:, m, n * NW:(n + 1) * NW]
                    pool.tensor_tensor(blk, blk, colb[i % 2][:, :], ALU.add).then_inc(pool_add, 1)

        @block.scalar
        def _(act):
            act.wait_ge(s_const, 16)
            act.activation(th[:, :], sc[:, 4:6], ACT.Tanh).then_inc(s_gate, 1)

            def std(t):
                act.wait_ge(var_ready, t + 1)
                act.activation(sd[:, 0:1], ve[:, 0:1], ACT.Sqrt).then_inc(std_ready, 1)

            def x_to_u8(t):
                act.wait_ge(qs_ready, t + 1)
                if t >= 1:
                    act.wait_ge(a_ready, t)
                act.activation(xu8[:, :], xg[(t // M) % 2][:, t % M, :], ACT.Identity,
                               scale=qs[:, 0:1], bias=qs[:, 1:2]).then_inc(xu8_ready, 1)

            def ctx_to_u8(q):
                act.wait_ge(c_in[q % 2], 16 * (q // 2 + 1))
                if q >= 2:
                    act.wait_ge(c_conv, q - 1)
                act.activation(cu8[q % 2][:, :, :], cst[q % 2][:, :, :], ACT.Identity,
                               scale=inv2, bias=z2).then_inc(cu8_ready, 1)

            def aT_copy(t):
                g, m = t // M, t % M
                act.wait_ge(tp_ready, t + 1)
                if g >= 2:
                    act.wait_ge(pe_unit, M * NB * (g - 1))
                act.activation(aT[g % 2][:, :, m * P:(m + 1) * P], tpa[:, :, :], ACT.Copy)\
                    .then_inc(aT_ready, 1)

            def evac(u):
                i, m = u // M, u % M
                t = M * (i // NB) + m
                act.wait_ge(pe_unit, u + 1)
                act.wait_ge(a_ready, t + 1)
                if u >= 2:
                    act.wait_ge(x1_ready, u - 1)
                act.activation(yev[u % 2][:, :], acc[m][:, :], ACT.Identity, scale=cg,
                               bias=crow[:, t:t + 1]).then_inc(evac_done, 1)

            def store_x1(i):
                g, n = i // NB, i % NB
                act.wait_ge(x1_ready, M * (i + 1))
                dst = x1s[g * GT:(g + 1) * GT, n * NW:(n + 1) * NW].rearrange("(m p) n -> p m n", p=P)
                act.dma_start(dst, xg[g % 2][:, :, n * NW:(n + 1) * NW]).then_inc(x1_stored[g % 2], 16)

            act.wait_ge(s_cst, 1)
            for t in range(M):
                std(t)
                x_to_u8(t)
                ctx_to_u8(t)
                aT_copy(t)
            for i in range(ITS):
                t, c = M + i, CTX_STEP.get(i)
                if i >= 1:
                    store_x1(i - 1)
                for m in range(M):
                    if c is not None:
                        ctx_to_u8(CP * c + m)
                    if m == 1 and t < TILES:
                        std(t)
                    if m == 2 and t < TILES:
                        x_to_u8(t)
                    evac(M * i + m)
                if t < TILES:
                    aT_copy(t)
                if i == ITS - NB:
                    act.wait_ge(var2_ready, 1)
                    act.activation(sd[:, :], ve[:, :], ACT.Sqrt).then_inc(std2_ready, 1)
                    for r in range(RING):
                        act.wait_ge(w_in[r], 16)
                        w = lead_piece(r)
                        act.activation(arh[:, 4 * r:4 * r + 4, :],
                                       wst[r][:, 0:w].rearrange("p (k n) -> p k n", n=AR), ACT.Copy)\
                            .then_inc(wh_ready, 1)
            store_x1(ITS - 1)

            def w_hi(g, X, lead=LEAD):
                s = X % RING
                act.wait_ge(w_in[s], g * (16 * WG // RING) + 16 * ((lead + X) // RING + 1))
                if lead == LEAD:
                    act.wait_ge(w_used, g * WG + (X - RING + 1))
                act.activation(wh[s][:, :], wst[s][:, :], ACT.Copy).then_inc(wh_ready, 1)

            def b_hi(r):
                act.wait_ge(w_in[r], 16 * 3)
                act.activation(bh[:, r * NW:(r + 1) * NW], wst[r][:, 0:NW], ACT.Copy).then_inc(wh_ready, 1)

            def h_hi(g, k):
                act.wait_ge(t_ready, g * K + (k + 1))
                act.activation(hh[:, k, :], tpb[k % 2], ACT.Copy).then_inc(hh_ready, 1)

            for k in range(K):
                h_hi(0, k)
                if k % 2:
                    i = k // 2
                    if i == 0:
                        act.wait_ge(x1_stored[1], 16 * NB * 2)
                    if i < RING:
                        w_hi(0, i, lead=RING)
                    else:
                        b_hi(i - RING)

            def group(g, last):
                act.wait_ge(lg_ready, g + 1)
                act.activation(ex[:, :, :], lg[:, :, :], ACT.Exp).then_inc(ex_ready, 1)
                for j in range(NB):
                    for q in range(WP):
                        if j == 0 and q == 3:
                            act.wait_ge(mt_ready, g + 1)
                            act.activation(mth[:, :], colp[:, :], ACT.Copy).then_inc(mth_ready, 1)
                        if j == 1 and q == 4 and not last:
                            act.wait_ge(var2_ready, g + 2)
                            act.activation(sd[:, :], ve[:, :], ACT.Sqrt).then_inc(std2_ready, 1)
                        if j == NB - 1 and not last:
                            h_hi(g + 1, 2 * q)
                            h_hi(g + 1, 2 * q + 1)
                        X = WP * j + RING + q
                        if not (last and X >= WG):
                            w_hi(g, X)
                    for m in range(M):
                        act.wait_ge(out_ready, g * ITS + (M * j + m + 1))
                        act.dma_start(rows(out, g, m, j), res[m][:, :]).then_inc(out_stored[m], 16)

            with act.Fori(0, G - 1) as g:
                group(g, False)
            group(G - 1, True)

        @block.vector
        def _(dve):
            link = Chain(dve, s_chain)
            dve.wait_ge(s_const, 16)
            link(dve.reciprocal(inv1, s1))
            link(dve.reciprocal(inv2, s2))
            link(dve.tensor_scalar(d1, z1, -1.0, MID, ALU.mult, ALU.add))
            link(dve.tensor_scalar(d2, z2, -1.0, MID, ALU.mult, ALU.add))
            dve.wait_ge(s_gate, 1)
            link(dve.tensor_scalar(cg, th[:, 0:1], s1, s2, ALU.mult, ALU.mult))
            link(dve.tensor_scalar(cd1, cg, d1, None, ALU.mult))
            link(dve.tensor_scalar(cd2, cg, d2, None, ALU.mult))
            dve.tensor_scalar(ckd, cd1, d2, float(D), ALU.mult, ALU.mult).then_inc(s_cst, 1)
            dve.wait_ge(s_cst, 1)

            def chunk_stats(chain, chunks, src):
                for c in range(D // NW):
                    chain(dve.bn_stats(chunks[:, 6 * c:6 * c + 6], src[:, c * NW:(c + 1) * NW]))

            def rstd(chain, w):
                chain(dve.reciprocal(rs[:, 0:w], sd[:, 0:w]))
                chain(dve.tensor_tensor(nt[:, 0:w], rs[:, 0:w], rs[:, 0:w], ALU.mult))
                chain(dve.tensor_tensor(nt[:, 0:w], nt[:, 0:w], ve[:, 0:w], ALU.mult))
                chain(dve.tensor_scalar(nt[:, 0:w], nt[:, 0:w], -0.5, 1.5, ALU.mult, ALU.add))
                chain(dve.tensor_tensor(rs[:, 0:w], rs[:, 0:w], nt[:, 0:w], ALU.mult))

            def x_stats(t):
                g, m = t // M, t % M
                dve.wait_ge(x_in[g % 2][m], 16 * (g // 2 + 1))
                chunk_stats(link, st[:, :], xg[g % 2][:, m, :])
                link(dve.bn_aggr(mv[:, 0, :], st[:, :]))
                dve.tensor_scalar(ve[:, 0:1], mv[:, 0, 1:2], EPS, None, ALU.add).then_inc(var_ready, 1)

            def x_scale(t):
                dve.wait_ge(std_ready, t + 1)
                rstd(link, 1)
                link(dve.tensor_scalar(qs[:, 0:1], rs[:, 0:1], inv1, None, ALU.mult))
                link(dve.tensor_scalar(qs[:, 2:3], mv[:, 0, 0:1], qs[:, 0:1], -1.0, ALU.mult, ALU.mult))
                dve.tensor_scalar(qs[:, 1:2], qs[:, 2:3], z1, None, ALU.add).then_inc(qs_ready, 1)

            def x_widen(t):
                dve.wait_ge(xu8_ready, t + 1)
                if t >= 1:
                    dve.wait_ge(tp_ready, t)
                link(dve.tensor_scalar(anat[:, :], xu8[:, :], -MID, 0.0, ALU.add, ALU.add,
                                       accum_out=asum[:, :]))
                dve.tensor_scalar(crow[:, t:t + 1], asum[:, :], cd2, ckd, ALU.mult, ALU.add)\
                    .then_inc(a_ready, 1)

            def ctx_widen(q):
                c, p = q // CP, q % CP
                n = c % NB
                dve.wait_ge(cu8_ready, q + 1)
                if c >= NB:
                    dve.wait_ge(pe_unit, M * (c + 1))
                dst = ctxq[:, n, PK * p:PK * (p + 1), :]
                dve.tensor_scalar(dst, cu8[q % 2][:, :, :], -MID, None, ALU.add).then_inc(c_conv, 1)
                dve.wait_ge(c_conv, q + 1)
                link(dve.tensor_tensor(half[:, :, :], dst[:, 0:2, :], dst[:, 2:4, :], ALU.add))
                to = csum[:, n, :] if p == 0 else quart[:, :]
                link(dve.tensor_tensor(to, half[:, 0, :], half[:, 1, :], ALU.add))
                if p:
                    ins = dve.tensor_tensor(csum[:, n, :], csum[:, n, :], quart[:, :], ALU.add)
                    if p == CP - 1:
                        ins.then_inc(block_ready, 1)
                    else:
                        link(ins)

            def col_term(i):
                dve.wait_ge(col_ready, i + 1)
                if i >= 2:
                    dve.wait_ge(pool_add, M * (i - 1))
                dve.tensor_scalar(colb[i % 2][:, :], colp[:, :], cd1, None, ALU.mult)\
                    .then_inc(colb_ready, 1)

            def x1_add(u):
                i, m = u // M, u % M
                g, n = i // NB, i % NB
                dve.wait_ge(evac_done, u + 1)
                dve.wait_ge(pool_add, u + 1)
                blk = xg[g % 2][:, m, n * NW:(n + 1) * NW]
                dve.tensor_tensor(blk, yev[u % 2][:, :], blk, ALU.add).then_inc(x1_ready, 1)

            for t in range(M):
                x_stats(t)
                x_scale(t)
                x_widen(t)
                ctx_widen(t)

            cb = Chain(dve, s_chain_b)

            def group_stats(chain, g, m):
                dve.wait_ge(g_in[m], g * 16 + 16)
                chunk_stats(chain, st2[:, m, :], xg[0][:, m, :])

            def group_mean_var(chain, m):
                chain(dve.bn_aggr(mv[:, m, :], st2[:, m, :]))

            def group_var(chain):
                dve.tensor_scalar(ve[:, :], mv[:, :, 1], EPS, None, ALU.add).then_inc(var2_ready, 1)

            def normalise(chain, m):
                blk = xg[0][:, m, :]
                ins = dve.tensor_scalar(blk, blk, mv[:, m, 0:1], rs[:, m:m + 1], ALU.subtract, ALU.mult)
                if m == M - 1:
                    ins.then_inc(xn_ready, 1)
                else:
                    chain(ins)

            for i in range(ITS):
                t, c = M + i, CTX_STEP.get(i)
                col_term(i)
                for m in range(M):
                    if c is not None:
                        ctx_widen(CP * c + m)
                    if m == 1 and t < TILES:
                        x_scale(t)
                    x1_add(M * i + m)
                    if m == 0 and t < TILES:
                        x_stats(t)
                    if m == 2 and t < TILES:
                        x_widen(t)
                    if i == ITS - NB:
                        group_stats(link, 0, m)
                        group_mean_var(link, m)
                if i == ITS - NB:
                    group_var(link)
                if i == ITS - NB + 1:
                    dve.wait_ge(std2_ready, 1)
                    rstd(link, M)
                    for m in range(M):
                        normalise(link, m)
                    for r in range(RING):
                        dve.wait_ge(wh_ready, r + 1)
                        w = lead_piece(r)
                        dve.tensor_tensor(arl[:, 4 * r:4 * r + 4, :],
                                          wst[r][:, 0:w].rearrange("p (k n) -> p k n", n=AR),
                                          arh[:, 4 * r:4 * r + 4, :].bitcast(F32), ALU.subtract)\
                            .then_inc(wl_ready, 1)

            def w_lo(g, X, lead=LEAD):
                s = X % RING
                dve.wait_ge(wh_ready, g * WG + (lead + X + 1))
                dve.tensor_tensor(wl[s][:, :], wst[s][:, :], wh[s][:, :].bitcast(F32), ALU.subtract)\
                    .then_inc(wl_ready, 1)

            def b_lo(r):
                dve.wait_ge(wh_ready, LEAD + r + 1)
                cols = slice(r * NW, (r + 1) * NW)
                dve.tensor_tensor(bl[:, cols], wst[r][:, 0:NW], bh[:, cols].bitcast(F32), ALU.subtract)\
                    .then_inc(wl_ready, 1)

            def h_lo(g, k):
                dve.wait_ge(hh_ready, g * K + (k + 1))
                dve.tensor_tensor(hl[:, k, :], tpb[k % 2], hh[:, k, :].bitcast(F32), ALU.subtract)\
                    .then_inc(hl_ready, 1)

            for k in range(K):
                h_lo(0, k)
                if k % 2:
                    i = k // 2
                    if i < RING:
                        w_lo(0, i, lead=RING)
                    else:
                        b_lo(i - RING)

            def router(chain, g):
                for m in range(M):
                    dve.wait_ge(ar_done, g * M + (m + 1))
                    dve.tensor_copy(mid[:, m, :], acc[m][:, 0:AR]).then_inc(ar_evac, 1)
                dve.wait_ge(ar_evac, g * M + M)
                L = mid[:, :, ER:AR]
                chain(dve.tensor_reduce(mx[:, :], L, AX.X, ALU.max))
                dve.tensor_tensor(lg[:, :, :], L, mx[:, :].unsqueeze(2).to_broadcast([P, M, E]),
                                  ALU.subtract).then_inc(lg_ready, 1)
                for m in range(M):
                    lj = mid[:, m, ER:AR].unsqueeze(1).to_broadcast([P, E, E])
                    le = mid[:, m, ER:AR].unsqueeze(2).to_broadcast([P, E, E])
                    chain(dve.tensor_tensor(rank[:, m, :, :], lj, le, ALU.is_gt))
                    chain(dve.tensor_tensor(rankeq[:, m, :, :], lj, le, ALU.is_equal))
                    chain(dve.tensor_tensor(rankeq[:, m, :, :], rankeq[:, m, :, :], tri[:, :, :], ALU.mult))
                chain(dve.tensor_tensor(rank[:, :, :, :], rank[:, :, :, :], rankeq[:, :, :, :], ALU.add))
                chain(dve.tensor_reduce(rk[:, :, :], rank[:, :, :, :], AX.X, ALU.add))
                dve.wait_ge(ex_ready, g + 1)
                chain(dve.scalar_tensor_tensor(out=wsel[:, :, :], in0=rk[:, :, :], scalar=float(TOP_K),
                                               in1=ex[:, :, :], op0=ALU.is_lt, op1=ALU.mult))
                chain(dve.tensor_reduce(den[:, :], wsel[:, :, :], AX.X, ALU.add))
                chain(dve.reciprocal(den[:, :], den[:, :]))
                chain(dve.scalar_tensor_tensor(out=wsel[:, :, :], in0=wsel[:, :, :], scalar=SCALING,
                                               in1=den[:, :].unsqueeze(2).to_broadcast([P, M, E]),
                                               op0=ALU.mult, op1=ALU.mult))
                for m in range(M):
                    ins = dve.tensor_tensor(mids[:, m, :, :],
                                            mid[:, m, 0:ER].rearrange("p (e r) -> p e r", r=R),
                                            wsel[:, m, :].unsqueeze(2).to_broadcast([P, E, R]), ALU.mult)
                    if m == M - 1:
                        ins.then_inc(mids_ready, 1)
                    else:
                        chain(ins)

            def group(g, last):
                chain = Chain(dve, s_chain_b, g * CHAIN_B)
                router(chain, g)
                for j in range(NB):
                    for q in range(WP):
                        if j == 0 and q == 3:
                            dve.wait_ge(mth_ready, g + 1)
                            dve.tensor_tensor(mtl[:, :], colp[:, :], mth[:, :].bitcast(F32), ALU.subtract)\
                                .then_inc(mtl_ready, 1)
                        if not last and j == 1:
                            if q < M:
                                group_stats(chain, g + 1, q)
                            if q == M + 1:
                                dve.wait_ge(std2_ready, g + 2)
                                rstd(chain, M)
                                for m in range(M):
                                    normalise(chain, m)
                        if j == NB - 1 and not last:
                            h_lo(g + 1, 2 * q)
                            h_lo(g + 1, 2 * q + 1)
                        X = WP * j + RING + q
                        if not (last and X >= WG):
                            w_lo(g, X)
                        if not last and j == 1 and q < M:
                            group_mean_var(chain, q)
                            if q == M - 1:
                                group_var(chain)
                    for m in range(M):
                        dve.wait_ge(acc_done, g * ITS + (M * j + m + 1))
                        dve.wait_ge(r_in[m], g * (16 * NB) + 16 * (j + 1))
                        dve.scalar_tensor_tensor(out=res[m][:, :], in0=acc[m][:, :], scalar=gate2,
                                                 in1=res[m][:, :], op0=ALU.mult, op1=ALU.add)\
                            .then_inc(out_ready, 1)
                assert last or chain.n == CHAIN_B, chain.n

            with dve.Fori(0, G - 1) as g:
                group(g, False)
            group(G - 1, True)

        @block.tensor
        def _(pe):
            pe.wait_ge(s_id, 7)

            def transpose_a(t):
                pe.wait_ge(a_ready, t + 1)
                if t >= 1:
                    pe.wait_ge(aT_ready, t)
                for k in range(K):
                    ins = pe.transpose(tpa[:, k, :], anat[:, k * P:(k + 1) * P], idb[:, :])
                ins.then_inc(tp_ready, 1)

            for t in range(M):
                transpose_a(t)
            for i in range(ITS):
                g, n = i // NB, i % NB
                pe.wait_ge(block_ready, NB * (g // 2) + n + 1)
                if i >= 1:
                    pe.wait_ge(colb_ready, i)
                pe.matmul(colp[:, :], ones[:, :], csum[:, n, :], start=True, stop=True).then_inc(col_ready, 1)
                for m in range(M):
                    u = M * i + m
                    pe.wait_ge(aT_ready, M * g + m + 1)
                    if i >= 1:
                        pe.wait_ge(evac_done, u - M + 1)
                    for k in range(K):
                        ins = pe.matmul(acc[m][:, :], aT[g % 2][:, k, m * P:(m + 1) * P], ctxq[:, n, k, :],
                                        start=(k == 0), stop=(k == K - 1))
                    ins.then_inc(pe_unit, 1)
                if M + i < TILES:
                    transpose_a(M + i)

            def three(out_, lh, ll, rh, rl, first, final):
                pe.matmul(out_, lh, rh, start=first, stop=False)
                pe.matmul(out_, lh, rl, start=False, stop=False)
                return pe.matmul(out_, ll, rh, start=False, stop=final)

            def transpose_h(g, k):
                if k == 0:
                    pe.wait_ge(xn_ready, g + 1)
                if not (isinstance(g, int) and k < 2):
                    pe.wait_ge(hl_ready, g * K + (k - 1))
                for m in range(M):
                    ins = pe.transpose(tpb[k % 2][:, m * P:(m + 1) * P], xg[0][:, m, k * P:(k + 1) * P],
                                       idf[:, :])
                ins.then_inc(t_ready, 1)

            def tok(m):
                return slice(m * P, (m + 1) * P)

            def ar_slice(g, k):
                if k == 0:
                    pe.wait_ge(wl_ready, RING)
                pe.wait_ge(hl_ready, g * K + (k + 1))
                for m in range(M):
                    if k == 0:
                        if isinstance(g, int):
                            pe.wait_ge(evac_done, M * (ITS - 1) + m + 1)
                        else:
                            pe.wait_ge(out_ready, g * ITS + (m + 1 - M))
                    ins = three(acc[m][:, 0:AR], hh[:, k, tok(m)], hl[:, k, tok(m)],
                                arh[:, k, :], arl[:, k, :], k == 0, k == K - 1)
                    if k == K - 1:
                        ins.then_inc(ar_done, 1)

            transpose_h(0, 0)
            transpose_h(0, 1)
            for k in range(K):
                ar_slice(0, k)
                if k + 2 < K:
                    transpose_h(0, k + 2)

            def group(g, last):
                for j in range(NB):
                    for q in range(WP):
                        X = WP * j + q
                        s = X % RING
                        pe.wait_ge(wl_ready, g * WG + (LEAD + X + 1))
                        for kk in range(WK):
                            k = WK * q + kk
                            cols = slice(kk * NW, (kk + 1) * NW)
                            for m in range(M):
                                if k == 0 and j == 0:
                                    pe.wait_ge(ar_evac, g * M + (m + 1))
                                elif k == 0:
                                    pe.wait_ge(out_ready, g * ITS + (M * (j - 1) + m + 1))
                                ins = three(acc[m][:, :], hh[:, k, tok(m)], hl[:, k, tok(m)],
                                            wh[s][:, cols], wl[s][:, cols], k == 0, False)
                            if kk == WK - 1:
                                ins.then_inc(w_used, 1)
                            if j == NB - 1 and not last:
                                transpose_h(g + 1, k)
                        if j == 0 and q == 3:
                            pe.wait_ge(mids_ready, g + 1)
                            for m in range(M):
                                ins = pe.transpose(colp[:, tok(m)],
                                                   mids[:, m, :, :].rearrange("p e r -> p (e r)"), idf[:, :])
                            ins.then_inc(mt_ready, 1)
                    cols = slice(j * NW, (j + 1) * NW)
                    if j == 0:
                        pe.wait_ge(mtl_ready, g + 1)
                    for m in range(M):
                        three(acc[m][:, :], mth[:, tok(m)], mtl[:, tok(m)], bh[:, cols], bl[:, cols],
                              False, True).then_inc(acc_done, 1)
                if not last:
                    for k in range(K):
                        ar_slice(g + 1, k)

            with pe.Fori(0, G - 1) as g:
                group(g, False)
            group(G - 1, True)


def kernel(x, ctx_4096, g_xattn, g_ffn, L0_xattn_x1_scale, L0_xattn_x1_zp, L0_xattn_x2_scale,
           L0_xattn_x2_zp, L0_ffn_base_W, L0_ffn_router_W, L0_ffn_lora_A, L0_ffn_lora_B):
    import numpy as np
    import concourse.bacc as bacc
    from concourse.bass_utils import run_bass_kernel_spmd

    scal = [L0_xattn_x1_scale, L0_xattn_x1_zp, L0_xattn_x2_scale, L0_xattn_x2_zp, g_xattn, g_ffn]
    lora_a = np.transpose(np.asarray(L0_ffn_lora_A), (1, 0, 2)).reshape(D, ER)
    arrays = {
        "in_x": np.asarray(x).reshape(TOK, D),
        "in_ctx": np.asarray(ctx_4096),
        "in_wt": np.asarray(L0_ffn_base_W).T,
        "in_ar": np.concatenate([lora_a, np.asarray(L0_ffn_router_W).T], axis=1),
        "in_lb": np.asarray(L0_ffn_lora_B).reshape(ER, D),
        "in_scal": np.broadcast_to(np.concatenate([np.asarray(s).reshape(1) for s in scal])[None, :], (P, 6)),
    }
    arrays = {n: np.ascontiguousarray(a) for n, a in arrays.items()}
    nc = bacc.Bacc("TRN2", target_bir_lowering=False, num_devices=1)
    args = [nc.dram_tensor(n, a.shape, F32, kind="ExternalInput").ap() for n, a in arrays.items()]
    args.append(nc.dram_tensor("x1_scratch", (TOK, D), F32, kind="Internal").ap())
    args.append(nc.dram_tensor("out_0", (TOK, D), F32, kind="ExternalOutput").ap())
    build(nc, *args)
    r = run_bass_kernel_spmd(nc, [arrays], core_ids=[0])
    return r.results[0]["out_0"].reshape(np.asarray(x).shape)
```

```python
import concourse.bass as bass
from concourse import mybir
from contextlib import ExitStack

F32 = mybir.dt.float32
F32R = mybir.dt.float32r
BF16 = mybir.dt.bfloat16
F16 = mybir.dt.float16
U8 = mybir.dt.uint8
ALU = mybir.AluOpType
ACT = mybir.ActivationFunctionType
AX = mybir.AxisListType

P = 128
D = 2048
TOK = 2048
K = D // P
NW = 512
NB = D // NW
GT = 512
G = TOK // GT
M = GT // P
TILES = G * M
ITS = G * NB
E, R = 8, 16
ER = E * R
AR = ER + E
TOP_K = 2
SCALING = 2.0
EPS = 1e-5
MID = 128.0
PK = 4
CP = K // PK
CS = 3
WK = 2
WP = K // WK
WG = NB * WP
RING = 4
LEAD = 2 * RING
CHAIN_B = 54
KIB = 1024

UNIT_AT = {4 + 2 * u if u < M else 7 + u: u for u in range(M * ITS)}
TILE_AT = {2 * t if t < M else 16 * (t // M) - 5 + 3 * (t % M): t for t in range(TILES)}
PIECE_AT = dict(zip([0, 1, 2, 3, 5, 7, 8, 9] + list(range(11, 19)) + [27 + 3 * e // 2 for e in range(16)],
                    range(2 * NB * CP)))
SLOTS = max(UNIT_AT) + 3
B0 = 57


class Chain:

    def __init__(self, eng, sem, base=0):
        self.eng, self.sem, self.base, self.n = eng, sem, base, 0

    def __call__(self, ins, wait=True):
        self.n += 1
        ins.then_inc(self.sem, 1)
        if wait:
            self.eng.wait_ge(self.sem, self.base + self.n)


def build(nc, x, ctx, wt, ar, lb, scal, x1s, out):
    es = ExitStack()
    with es:
        top = nc.sbuf_base

        def at(name, off, shape, dt):
            return nc.alloc_sbuf_tensor_at(name, shape, dt, offset=off)

        def psum(name, shape, dt):
            return es.enter_context(nc.psum_tensor(name, shape, dt))

        def sem(name):
            return es.enter_context(nc.semaphore(name))

        XG0 = (top + 31) // 32 * 32
        XG1 = XG0 + 32 * KIB
        AT0 = XG1 + 32 * KIB
        AT1 = AT0 + 16 * KIB
        CTX = AT1 + 16 * KIB
        CST = CTX + 64 * KIB
        SMALL = CST + 28 * KIB
        LAST = SMALL + 22 * KIB
        xg = [at("x_group_even", XG0, [P, M, D], F32), at("x_group_odd", XG1, [P, M, D], F32)]
        aT = [at("aT_even", AT0, [P, K, GT], BF16), at("aT_odd", AT1, [P, K, GT], BF16)]
        ctxq = at("ctx_quant", CTX, [P, NB, K, NW], BF16)
        cst = [at(f"ctx_stage{s}", CST + 8 * KIB * s, [P, PK, NW], F32) for s in range(CS)]
        cu8 = [at(f"ctx_u8_{s}", CST + 24 * KIB + 2 * KIB * s, [P, PK, NW], U8) for s in range(2)]
        anat = at("a_rows", SMALL, [P, D], BF16)
        xu8 = at("x_u8", SMALL + 4 * KIB, [P, D], U8)
        csum = at("ctx_part_sums", SMALL + 6 * KIB, [P, NB, NW], F16)
        tree = at("ctx_tree_sums", SMALL + 10 * KIB, [P, K // 2, NW], F16)
        colb = [at(f"col_term{s}", SMALL + 18 * KIB + 2 * KIB * s, [P, NW], F32) for s in range(2)]
        wst = [at(f"w_stage{s}", AT0 + 4 * KIB * s, [P, WK * NW], F32) for s in range(RING)]
        wh = [at(f"w_hi{s}", XG1 + 8 * KIB * s, [P, WK * NW], F32R) for s in range(RING)]
        wl = [at(f"w_lo{s}", XG1 + 8 * KIB * s + 4 * KIB, [P, WK * NW], F32R) for s in range(RING)]
        hh = at("hT_hi", CTX, [P, K, GT], F32R)
        hl = at("hT_lo", CTX + 32 * KIB, [P, K, GT], F32R)
        arw = at("ar_hi_lo", CST, [P, K, 2, AR], F32R)
        bh = at("b_hi", AT1, [P, D], F32R)
        bl = at("b_lo", AT1 + 8 * KIB, [P, D], F32R)
        res = [at(f"residual{m}", SMALL + 2 * KIB * m, [P, NW], F32) for m in range(M)]
        mids = at("mid_scaled", SMALL + 8 * KIB, [P, M, E, R], F32)
        mth = at("midT_hi", SMALL + 10 * KIB, [P, GT], F32R)
        mtl = at("midT_lo", SMALL + 12 * KIB, [P, GT], F32R)
        mid = at("mid", SMALL + 14 * KIB, [P, M, AR], F32)
        rank = at("router_rank", SMALL + 17 * KIB, [P, M, E, E], F32)
        rankeq = at("router_rank_eq", SMALL + 18 * KIB, [P, M, E, E], F32)
        o = [LAST]

        def keep(name, shape, dt, size):
            off, o[0] = o[0], o[0] + (size + 31) // 32 * 32
            return at(name, off, shape, dt)

        idf = keep("identity_f32", [P, P], F32, 512)
        idb = keep("identity_bf16", [P, P], BF16, 256)
        ones = keep("ones_f16", [P, P], F16, 256)
        tri = keep("earlier_expert", [P, E, E], F32, 256)
        sc = keep("scalars", [P, 6], F32, 24)
        th = keep("gates", [P, 2], F32, 8)
        cst_ = keep("constants", [P, 8], F32, 32)
        st = keep("bn_chunks", [P, 4 * 6], F32, 96)
        st2 = keep("bn_chunks_group", [P, M, 4 * 6], F32, 384)
        mv = keep("mean_var", [P, M, 2], F32, 32)
        ve = keep("var_eps", [P, M], F32, 16)
        sd = keep("std", [P, M], F32, 16)
        rs = keep("rstd", [P, M], F32, 16)
        nt = keep("newton", [P, M], F32, 16)
        qs = keep("quant_scale_bias", [P, 4], F32, 16)
        asum = keep("a_row_sum", [P, 1], F32, 4)
        crow = keep("row_terms", [P, TILES], F32, 64)
        lg = keep("logits_minus_max", [P, M, E], F32, 128)
        ex = keep("exp_logits", [P, M, E], F32, 128)
        rk = keep("rank", [P, M, E], F32, 128)
        wsel = keep("expert_weights", [P, M, E], F32, 128)
        mx = keep("logit_max", [P, M], F32, 16)
        den = keep("weight_sum", [P, M], F32, 16)
        assert o[0] <= nc.sbuf_usable_end, (o[0], nc.sbuf_usable_end)

        s1, z1, s2, z2 = (sc[:, i:i + 1] for i in range(4))
        inv1, inv2, cg, d1, d2, cd1, cd2, ckd = (cst_[:, i:i + 1] for i in range(8))
        gate2 = th[:, 1:2]

        acc = [psum(f"acc{m}", [P, NW], F32) for m in range(M)]
        tpa = psum("aT_psum", [P, K, P], BF16)
        tpb = [tpa[:, 8 * s:8 * s + 8, :].rearrange("p a b -> p (a b)").bitcast(F32) for s in range(2)]
        colp = psum("col_psum", [P, NW], F32)
        acc0b = psum("acc0_odd", [P, NW], F32)

        def bank(j, m):
            return acc0b if m == 0 and j % 2 else acc[m]

        s_const = sem("s_const")
        s_gate = sem("s_gate")
        s_cst = sem("s_cst")
        s_id = sem("s_id")
        s_chain = sem("s_chain")
        x_in = [[sem(f"x_in{a}{m}") for m in range(M)] for a in range(2)]
        var_ready = sem("var_ready")
        std_ready = sem("std_ready")
        qs_ready = sem("qs_ready")
        xu8_ready = sem("xu8_ready")
        a_ready = sem("a_ready")
        tp_ready = sem("tp_ready")
        aT_ready = sem("aT_ready")
        xr_ready = sem("xr_ready")
        c_in = [sem(f"c_in{s}") for s in range(CS)]
        cu8_ready = sem("cu8_ready")
        c_conv = sem("c_conv")
        block_ready = sem("block_ready")
        col_ready = sem("col_ready")
        colb_ready = sem("colb_ready")
        pool_add = sem("pool_add")
        pe_unit = sem("pe_unit")
        x1_ready = sem("x1_ready")
        x1_stored = [sem(f"x1_stored{a}") for a in range(2)]
        s_chain_b = sem("s_chain_b")
        g_in = [sem(f"g_in{m}") for m in range(M)]
        xn_ready = sem("xn_ready")
        var2_ready = sem("var2_ready")
        std2_ready = sem("std2_ready")
        w_in = [sem(f"w_in{s}") for s in range(RING)]
        wh_ready = sem("wh_ready")
        wl_ready = sem("wl_ready")
        w_used = sem("w_used")
        t_ready = sem("t_ready")
        hh_ready = sem("hh_ready")
        hl_ready = sem("hl_ready")
        ar_done = sem("ar_done")
        ar_evac = sem("ar_evac")
        lg_ready = sem("lg_ready")
        ex_ready = sem("ex_ready")
        mids_ready = sem("mids_ready")
        mt_ready = sem("mt_ready")
        mth_ready = sem("mth_ready")
        mtl_ready = sem("mtl_ready")
        acc_done = sem("acc_done")
        r_in = [sem(f"r_in{m}") for m in range(M)]
        out_ready = sem("out_ready")
        out_stored = [sem(f"out_stored{m}") for m in range(M)]

        def rows(t, g, m, n):
            return t[bass.ds(g * GT + m * P, P), n * NW:(n + 1) * NW]

        def w_piece(X):
            Y = X % WG
            k0, n = WK * (Y % WP), Y // WP
            return wt[k0 * P:(k0 + WK) * P, n * NW:(n + 1) * NW].rearrange("(k p) n -> p k n", p=P)

        def lead_piece(i):
            return 4 * AR if i < RING else NW

        block = es.enter_context(nc.Block())

        @block.sync
        def _(sp):
            def load_x(t):
                g, m = t // M, t % M
                if g >= 2:
                    sp.wait_ge(x1_stored[g % 2], 16 * NB * (g // 2))
                sp.dma_start(xg[g % 2][:, m, :], x[t * P:(t + 1) * P, :]).then_inc(x_in[g % 2][m], 16)

            def load_ctx(q):
                c, p = q // CP, q % CP
                b, n = c // NB, c % NB
                if q >= CS:
                    sp.wait_ge(cu8_ready, q - CS + 1)
                src = ctx[b, p * PK * P:(p + 1) * PK * P, n * NW:(n + 1) * NW]
                sp.dma_start(cst[q % CS][:, :, :], src.rearrange("(k p) n -> p k n", p=P))\
                    .then_inc(c_in[q % CS], 16)

            def load_group(g):
                for m in range(M):
                    sp.dma_start(xg[0][:, m, :], x1s[bass.ds(g * GT + m * P, P), :])\
                        .then_inc(g_in[m], 16)

            def load_lead(i, slot):
                w = lead_piece(i)
                if i < RING:
                    src = ar[4 * i * P:4 * (i + 1) * P, :].rearrange("(k p) n -> p k n", p=P)
                    dst = wst[slot][:, 0:w].rearrange("p (k n) -> p k n", n=AR)
                else:
                    src, dst = lb[:, (i - RING) * NW:(i - RING + 1) * NW], wst[slot][:, 0:w]
                sp.dma_start(dst, src).then_inc(w_in[slot], 16)

            def load_w(X):
                sp.dma_start(wst[X % RING][:, :].rearrange("p (k n) -> p k n", n=NW), w_piece(X))\
                    .then_inc(w_in[X % RING], 16)

            def load_res(g, n):
                for m in range(M):
                    sp.dma_start(res[m][:, :], rows(x1s, g, m, n)).then_inc(r_in[m], 16)

            sp.dma_start(sc[:, :], scal).then_inc(s_const, 16)
            load_x(0)
            load_ctx(0)
            for s in range(1, SLOTS):
                if s in PIECE_AT:
                    load_ctx(PIECE_AT[s])
                if s in TILE_AT:
                    load_x(TILE_AT[s])
                if s == B0:
                    sp.wait_ge(x1_stored[0], 16 * NB * 2)
                    load_group(0)
                    sp.wait_ge(pe_unit, M * NB * (G - 1))
                    for r in range(RING):
                        load_lead(r, r)
            for a in range(2):
                sp.wait_ge(x1_stored[a], 16 * NB * 2)
            for X in range(RING):
                sp.wait_ge(wl_ready, X + 1)
                load_w(X)
            load_res(0, 0)
            for r in range(RING):
                sp.wait_ge(wl_ready, RING + r + 1)
                load_lead(RING + r, r)

            def group(g, last):
                for j in range(NB):
                    for q in range(WP):
                        X = WP * j + RING + q
                        if not (last and X >= WG):
                            sp.wait_ge(wl_ready, g * WG + (LEAD + X - RING + 1))
                            load_w(X)
                        if j == 0 and q == 0 and not last:
                            sp.wait_ge(t_ready, g * K + K)
                            load_group(g + 1)
                    if not (last and j == NB - 1):
                        for m in range(M):
                            sp.wait_ge(out_stored[m], g * (16 * NB) + 16 * (j + 1))
                        if j < NB - 1:
                            load_res(g, j + 1)
                        else:
                            load_res(g + 1, 0)

            with sp.Fori(0, G - 1) as g:
                group(g, False)
            group(G - 1, True)
            for m in range(M):
                sp.wait_ge(out_stored[m], 16 * ITS)

        @block.gpsimd
        def _(pool):
            pool.memset(idf[:, :], 0.0).then_inc(s_id, 1)
            pool.memset(idb[:, :], 0.0).then_inc(s_id, 1)
            pool.memset(ones[:, :], 1.0).then_inc(s_id, 1)
            pool.memset(tri[:, :, :], 1.0).then_inc(s_id, 1)
            pool.wait_ge(s_id, 4)
            for t in (idf, idb):
                pool.affine_select(out=t[:, :], in_=t[:, :], compare_op=ALU.not_equal, fill=1.0, base=0,
                                   pattern=[[-1, P]], channel_multiplier=1).then_inc(s_id, 1)
            pool.affine_select(out=tri[:, :, :], in_=tri[:, :, :], compare_op=ALU.is_gt, fill=0.0, base=0,
                               pattern=[[1, E], [-1, E]], channel_multiplier=0).then_inc(s_id, 1)

            def ctx_widen(q):
                c, p = q // CP, q % CP
                pool.wait_ge(cu8_ready, q + 1)
                if c >= NB:
                    pool.wait_ge(pe_unit, M * (c + 1))
                pool.tensor_scalar(ctxq[:, c % NB, PK * p:PK * (p + 1), :], cu8[q % 2][:, :, :], -MID, 1.0,
                                   ALU.add, ALU.mult).then_inc(c_conv, 1)

            def row_term(t):
                pool.wait_ge(a_ready, t + 1)
                tile = xg[(t // M) % 2][:, t % M, :]
                pool.tensor_scalar(tile, tile, crow[:, t:t + 1], 1.0, ALU.add, ALU.mult).then_inc(xr_ready, 1)

            def add_col_term(u):
                i, m = u // M, u % M
                g, n = i // NB, i % NB
                pool.wait_ge(colb_ready, i + 1)
                pool.wait_ge(xr_ready, M * g + m + 1)
                blk = xg[g % 2][:, m, n * NW:(n + 1) * NW]
                pool.tensor_tensor(blk, blk, colb[i % 2][:, :], ALU.add).then_inc(pool_add, 1)

            for s in range(SLOTS):
                if s in PIECE_AT:
                    ctx_widen(PIECE_AT[s])
                if s - 3 in TILE_AT:
                    row_term(TILE_AT[s - 3])
                if s - 1 in UNIT_AT:
                    add_col_term(UNIT_AT[s - 1])

        @block.scalar
        def _(act):
            act.wait_ge(s_const, 16)
            act.activation(th[:, :], sc[:, 4:6], ACT.Tanh).then_inc(s_gate, 1)

            def std(t):
                act.wait_ge(var_ready, t + 1)
                act.activation(sd[:, 0:1], ve[:, 0:1], ACT.Sqrt).then_inc(std_ready, 1)

            def x_to_u8(t):
                act.wait_ge(qs_ready, t + 1)
                if t >= 1:
                    act.wait_ge(a_ready, t)
                act.activation(xu8[:, :], xg[(t // M) % 2][:, t % M, :], ACT.Identity,
                               scale=qs[:, 0:1], bias=qs[:, 1:2]).then_inc(xu8_ready, 1)

            def ctx_to_u8(q):
                act.wait_ge(c_in[q % CS], 16 * (q // CS + 1))
                if q >= 2:
                    act.wait_ge(c_conv, q - 1)
                act.activation(cu8[q % 2][:, :, :], cst[q % CS][:, :, :], ACT.Identity,
                               scale=inv2, bias=z2).then_inc(cu8_ready, 1)

            def aT_copy(t):
                g, m = t // M, t % M
                act.wait_ge(tp_ready, t + 1)
                if g >= 2:
                    act.wait_ge(pe_unit, M * NB * (g - 1))
                act.activation(aT[g % 2][:, :, m * P:(m + 1) * P], tpa[:, :, :], ACT.Copy)\
                    .then_inc(aT_ready, 1)

            def store_x1(i):
                g, n = i // NB, i % NB
                act.wait_ge(x1_ready, M * (i + 1))
                dst = x1s[g * GT:(g + 1) * GT, n * NW:(n + 1) * NW].rearrange("(m p) n -> p m n", p=P)
                act.dma_start(dst, xg[g % 2][:, :, n * NW:(n + 1) * NW]).then_inc(x1_stored[g % 2], 16)

            act.wait_ge(s_cst, 1)
            for s in range(SLOTS):
                if s in PIECE_AT:
                    ctx_to_u8(PIECE_AT[s])
                if s - 1 in TILE_AT:
                    x_to_u8(TILE_AT[s - 1])
                if s - 3 in TILE_AT:
                    aT_copy(TILE_AT[s - 3])
                if s in TILE_AT:
                    std(TILE_AT[s])
                if UNIT_AT.get(s - 2, 0) % M == M - 1:
                    store_x1(UNIT_AT[s - 2] // M)
                if s == B0 + M:
                    act.wait_ge(var2_ready, 1)
                    act.activation(sd[:, :], ve[:, :], ACT.Sqrt).then_inc(std2_ready, 1)
                if s == B0 + M + 2:
                    for r in range(RING):
                        act.wait_ge(w_in[r], 16)
                        w = lead_piece(r)
                        act.activation(arw[:, 4 * r:4 * r + 4, 0, :],
                                       wst[r][:, 0:w].rearrange("p (k n) -> p k n", n=AR), ACT.Copy)\
                            .then_inc(wh_ready, 1)

            def w_hi(g, X, lead=LEAD):
                s = X % RING
                act.wait_ge(w_in[s], g * (16 * WG // RING) + 16 * ((lead + X) // RING + 1))
                if lead == LEAD:
                    act.wait_ge(w_used, g * WG + (X - RING + 1))
                act.activation(wh[s][:, :], wst[s][:, :], ACT.Copy).then_inc(wh_ready, 1)

            def b_hi(r):
                act.wait_ge(w_in[r], 16 * 3)
                act.activation(bh[:, r * NW:(r + 1) * NW], wst[r][:, 0:NW], ACT.Copy).then_inc(wh_ready, 1)

            def h_hi(g, k):
                act.wait_ge(t_ready, g * K + (k + 1))
                act.activation(hh[:, k, :], tpb[k % 2], ACT.Copy).then_inc(hh_ready, 1)

            for k in range(K):
                h_hi(0, k)
                if k % 2:
                    i = k // 2
                    if i == 0:
                        act.wait_ge(x1_stored[1], 16 * NB * 2)
                    if i < RING:
                        w_hi(0, i, lead=RING)
                    else:
                        b_hi(i - RING)

            def group(g, last):
                act.wait_ge(lg_ready, g + 1)
                act.activation(ex[:, :, :], lg[:, :, :], ACT.Exp).then_inc(ex_ready, 1)
                for j in range(NB):
                    for q in range(WP):
                        if j == 0 and q == 3:
                            act.wait_ge(mt_ready, g + 1)
                            act.activation(mth[:, :], colp[:, :], ACT.Copy).then_inc(mth_ready, 1)
                        if j == 1 and q == 4 and not last:
                            act.wait_ge(var2_ready, g + 2)
                            act.activation(sd[:, :], ve[:, :], ACT.Sqrt).then_inc(std2_ready, 1)
                        if j == NB - 1 and not last:
                            h_hi(g + 1, 2 * q)
                            h_hi(g + 1, 2 * q + 1)
                        X = WP * j + RING + q
                        if not (last and X >= WG):
                            w_hi(g, X)
                    for m in range(M):
                        act.wait_ge(out_ready, g * ITS + (M * j + m + 1))
                        act.dma_start(rows(out, g, m, j), res[m][:, :]).then_inc(out_stored[m], 16)

            with act.Fori(0, G - 1) as g:
                group(g, False)
            group(G - 1, True)

        @block.vector
        def _(dve):
            link = Chain(dve, s_chain)
            dve.wait_ge(s_const, 16)
            link(dve.reciprocal(inv1, s1))
            link(dve.reciprocal(inv2, s2))
            link(dve.tensor_scalar(d1, z1, -1.0, MID, ALU.mult, ALU.add))
            link(dve.tensor_scalar(d2, z2, -1.0, MID, ALU.mult, ALU.add))
            dve.wait_ge(s_gate, 1)
            link(dve.tensor_scalar(cg, th[:, 0:1], s1, s2, ALU.mult, ALU.mult))
            link(dve.tensor_scalar(cd1, cg, d1, None, ALU.mult))
            link(dve.tensor_scalar(cd2, cg, d2, None, ALU.mult))
            dve.tensor_scalar(ckd, cd1, d2, float(D), ALU.mult, ALU.mult).then_inc(s_cst, 1)
            dve.wait_ge(s_cst, 1)

            def chunk_stats(chain, chunks, src):
                for c in range(D // NW):
                    chain(dve.bn_stats(chunks[:, 6 * c:6 * c + 6], src[:, c * NW:(c + 1) * NW]), wait=c == D // NW - 1)

            def rstd(chain, w):
                chain(dve.reciprocal(rs[:, 0:w], sd[:, 0:w]))
                if w == 1:
                    chain(dve.scalar_tensor_tensor(out=nt[:, 0:1], in0=rs[:, 0:1], scalar=rs[:, 0:1],
                                                   in1=ve[:, 0:1], op0=ALU.mult, op1=ALU.mult))
                else:
                    chain(dve.tensor_tensor(nt[:, 0:w], rs[:, 0:w], rs[:, 0:w], ALU.mult))
                    chain(dve.tensor_tensor(nt[:, 0:w], nt[:, 0:w], ve[:, 0:w], ALU.mult))
                chain(dve.tensor_scalar(nt[:, 0:w], nt[:, 0:w], -0.5, 1.5, ALU.mult, ALU.add))
                chain(dve.tensor_tensor(rs[:, 0:w], rs[:, 0:w], nt[:, 0:w], ALU.mult))

            def x_stats(t):
                g, m = t // M, t % M
                dve.wait_ge(x_in[g % 2][m], 16 * (g // 2 + 1))
                chunk_stats(link, st[:, :], xg[g % 2][:, m, :])
                link(dve.bn_aggr(mv[:, 0, :], st[:, :]))
                dve.tensor_scalar(ve[:, 0:1], mv[:, 0, 1:2], EPS, None, ALU.add).then_inc(var_ready, 1)

            def x_scale(t):
                dve.wait_ge(std_ready, t + 1)
                rstd(link, 1)
                link(dve.tensor_scalar(qs[:, 0:1], rs[:, 0:1], inv1, None, ALU.mult))
                dve.scalar_tensor_tensor(out=qs[:, 1:2], in0=mv[:, 0, 0:1], scalar=qs[:, 0:1], in1=z1,
                                         op0=ALU.mult, op1=ALU.subtract, reverse1=True).then_inc(qs_ready, 1)

            def x_widen(t):
                dve.wait_ge(xu8_ready, t + 1)
                if t >= 1:
                    dve.wait_ge(tp_ready, t)
                link(dve.tensor_scalar(anat[:, :], xu8[:, :], -MID, 0.0, ALU.add, ALU.add,
                                       accum_out=asum[:, :]))
                dve.tensor_scalar(crow[:, t:t + 1], asum[:, :], cd2, ckd, ALU.mult, ALU.add)\
                    .then_inc(a_ready, 1)

            def ctx_sums(c):
                dve.wait_ge(c_conv, CP * (c + 1))
                src, w = ctxq[:, c % NB, :, :], K // 2
                while w:
                    dst = tree[:, 0:w, :] if w > 1 else csum[:, c % NB, :].unsqueeze(1)
                    ins = dve.tensor_tensor(dst, src[:, 0:w, :], src[:, w:2 * w, :], ALU.add)
                    if w > 1:
                        link(ins)
                    else:
                        ins.then_inc(block_ready, 1)
                    src, w = tree, w // 2

            def col_term(i):
                dve.wait_ge(col_ready, i + 1)
                if i >= 2:
                    dve.wait_ge(pool_add, M * (i - 1))
                dve.tensor_scalar(colb[i % 2][:, :], colp[:, :], cd1, None, ALU.mult)\
                    .then_inc(colb_ready, 1)

            def evac(u):
                i, m = u // M, u % M
                g, n = i // NB, i % NB
                dve.wait_ge(pe_unit, u + 1)
                dve.wait_ge(pool_add, u + 1)
                blk = xg[g % 2][:, m, n * NW:(n + 1) * NW]
                dve.scalar_tensor_tensor(out=blk, in0=acc[m][:, :], scalar=cg, in1=blk, op0=ALU.mult,
                                         op1=ALU.add).then_inc(x1_ready, 1)

            def group_stats(chain, g, m):
                dve.wait_ge(g_in[m], g * 16 + 16)
                chunk_stats(chain, st2[:, m, :], xg[0][:, m, :])

            def group_mean_var(chain, m):
                chain(dve.bn_aggr(mv[:, m, :], st2[:, m, :]))

            def group_var(chain):
                dve.tensor_scalar(ve[:, :], mv[:, :, 1], EPS, None, ALU.add).then_inc(var2_ready, 1)

            def normalise(chain, m):
                blk = xg[0][:, m, :]
                ins = dve.tensor_scalar(blk, blk, mv[:, m, 0:1], rs[:, m:m + 1], ALU.subtract, ALU.mult)
                if m == M - 1:
                    ins.then_inc(xn_ready, 1)
                else:
                    chain(ins)

            for s in range(SLOTS):
                if UNIT_AT.get(s - 1, 1) % M == 0:
                    col_term(UNIT_AT[s - 1] // M)
                if s - 2 in UNIT_AT:
                    evac(UNIT_AT[s - 2])
                if s - 1 in TILE_AT:
                    x_scale(TILE_AT[s - 1])
                if s - 2 in TILE_AT:
                    x_widen(TILE_AT[s - 2])
                if s in TILE_AT:
                    x_stats(TILE_AT[s])
                if PIECE_AT.get(s - 1, 0) % CP == CP - 1:
                    ctx_sums(PIECE_AT[s - 1] // CP)
                if B0 + 1 <= s <= B0 + M:
                    group_stats(link, 0, s - B0 - 1)
                    group_mean_var(link, s - B0 - 1)
                if s == B0 + M:
                    group_var(link)
                if s == B0 + M + 1:
                    dve.wait_ge(std2_ready, 1)
                    rstd(link, M)
                if B0 + M + 1 <= s <= B0 + 2 * M:
                    normalise(link, s - B0 - M - 1)
                if s == B0 + 2 * M + 1:
                    for r in range(RING):
                        dve.wait_ge(wh_ready, r + 1)
                        w = lead_piece(r)
                        dve.tensor_tensor(arw[:, 4 * r:4 * r + 4, 1, :],
                                          wst[r][:, 0:w].rearrange("p (k n) -> p k n", n=AR),
                                          arw[:, 4 * r:4 * r + 4, 0, :].bitcast(F32), ALU.subtract)\
                            .then_inc(wl_ready, 1)

            def w_lo(g, X, lead=LEAD):
                s = X % RING
                dve.wait_ge(wh_ready, g * WG + (lead + X + 1))
                dve.tensor_tensor(wl[s][:, :], wst[s][:, :], wh[s][:, :].bitcast(F32), ALU.subtract)\
                    .then_inc(wl_ready, 1)

            def b_lo(r):
                dve.wait_ge(wh_ready, LEAD + r + 1)
                cols = slice(r * NW, (r + 1) * NW)
                dve.tensor_tensor(bl[:, cols], wst[r][:, 0:NW], bh[:, cols].bitcast(F32), ALU.subtract)\
                    .then_inc(wl_ready, 1)

            def h_lo(g, k):
                dve.wait_ge(hh_ready, g * K + (k + 1))
                dve.tensor_tensor(hl[:, k, :], tpb[k % 2], hh[:, k, :].bitcast(F32), ALU.subtract)\
                    .then_inc(hl_ready, 1)

            for k in range(K):
                h_lo(0, k)
                if k % 2:
                    i = k // 2
                    if i < RING:
                        w_lo(0, i, lead=RING)
                    else:
                        b_lo(i - RING)

            def router(chain, g):
                for m in range(M):
                    dve.wait_ge(ar_done, g * M + (m + 1))
                    chain(dve.tensor_copy(mid[:, m, :], acc[m][:, 0:AR]), wait=m == M - 1)
                for m in range(M):
                    dve.tensor_tensor(mid[:, m, :], acc[m][:, AR:2 * AR], mid[:, m, :], ALU.add)\
                        .then_inc(ar_evac, 1)
                dve.wait_ge(ar_evac, g * M + M)
                L = mid[:, :, ER:AR]
                chain(dve.tensor_reduce(mx[:, :], L, AX.X, ALU.max))
                dve.tensor_tensor(lg[:, :, :], L, mx[:, :].unsqueeze(2).to_broadcast([P, M, E]),
                                  ALU.subtract).then_inc(lg_ready, 1)
                for m in range(M):
                    lj = mid[:, m, ER:AR].unsqueeze(1).to_broadcast([P, E, E])
                    le = mid[:, m, ER:AR].unsqueeze(2).to_broadcast([P, E, E])
                    chain(dve.tensor_tensor(rank[:, m, :, :], lj, le, ALU.is_gt))
                    chain(dve.tensor_tensor(rankeq[:, m, :, :], lj, le, ALU.is_equal))
                    chain(dve.tensor_tensor(rankeq[:, m, :, :], rankeq[:, m, :, :], tri[:, :, :], ALU.mult))
                chain(dve.tensor_tensor(rank[:, :, :, :], rank[:, :, :, :], rankeq[:, :, :, :], ALU.add))
                chain(dve.tensor_reduce(rk[:, :, :], rank[:, :, :, :], AX.X, ALU.add))
                dve.wait_ge(ex_ready, g + 1)
                chain(dve.scalar_tensor_tensor(out=wsel[:, :, :], in0=rk[:, :, :], scalar=float(TOP_K),
                                               in1=ex[:, :, :], op0=ALU.is_lt, op1=ALU.mult))
                chain(dve.tensor_reduce(den[:, :], wsel[:, :, :], AX.X, ALU.add))
                chain(dve.reciprocal(den[:, :], den[:, :]))
                chain(dve.scalar_tensor_tensor(out=wsel[:, :, :], in0=wsel[:, :, :], scalar=SCALING,
                                               in1=den[:, :].unsqueeze(2).to_broadcast([P, M, E]),
                                               op0=ALU.mult, op1=ALU.mult))
                for m in range(M):
                    ins = dve.tensor_tensor(mids[:, m, :, :],
                                            mid[:, m, 0:ER].rearrange("p (e r) -> p e r", r=R),
                                            wsel[:, m, :].unsqueeze(2).to_broadcast([P, E, R]), ALU.mult)
                    if m == M - 1:
                        ins.then_inc(mids_ready, 1)
                    else:
                        chain(ins)

            def group(g, last):
                chain = Chain(dve, s_chain_b, g * CHAIN_B)
                router(chain, g)
                for j in range(NB):
                    for q in range(WP):
                        if j == 0 and q == 3:
                            dve.wait_ge(mth_ready, g + 1)
                            dve.tensor_tensor(mtl[:, :], colp[:, :], mth[:, :].bitcast(F32), ALU.subtract)\
                                .then_inc(mtl_ready, 1)
                        if not last and j == 1:
                            if q < M:
                                group_stats(chain, g + 1, q)
                            if q == M + 1:
                                dve.wait_ge(std2_ready, g + 2)
                                rstd(chain, M)
                                for m in range(M):
                                    normalise(chain, m)
                        if j == NB - 1 and not last:
                            h_lo(g + 1, 2 * q)
                            h_lo(g + 1, 2 * q + 1)
                        X = WP * j + RING + q
                        if not (last and X >= WG):
                            w_lo(g, X)
                        if not last and j == 1 and q < M:
                            group_mean_var(chain, q)
                            if q == M - 1:
                                group_var(chain)
                    for m in range(M):
                        dve.wait_ge(acc_done, g * ITS + (M * j + m + 1))
                        dve.wait_ge(r_in[m], g * (16 * NB) + 16 * (j + 1))
                        dve.scalar_tensor_tensor(out=res[m][:, :], in0=bank(j, m)[:, :], scalar=gate2,
                                                 in1=res[m][:, :], op0=ALU.mult, op1=ALU.add)\
                            .then_inc(out_ready, 1)
                assert last or chain.n == CHAIN_B, chain.n

            with dve.Fori(0, G - 1) as g:
                group(g, False)
            group(G - 1, True)

        @block.tensor
        def _(pe):
            pe.wait_ge(s_id, 7)

            def transpose_a(t):
                pe.wait_ge(a_ready, t + 1)
                if t >= 1:
                    pe.wait_ge(aT_ready, t)
                for k in range(K):
                    ins = pe.transpose(tpa[:, k, :], anat[:, k * P:(k + 1) * P], idb[:, :])
                ins.then_inc(tp_ready, 1)

            def unit(u):
                i, m = u // M, u % M
                g, n = i // NB, i % NB
                c = NB * (g // 2) + n
                pe.wait_ge(c_conv, CP * (c + 1))
                pe.wait_ge(aT_ready, M * g + m + 1)
                if i >= 1:
                    pe.wait_ge(x1_ready, u - M + 1)
                for k in range(K):
                    ins = pe.matmul(acc[m][:, :], aT[g % 2][:, k, m * P:(m + 1) * P], ctxq[:, n, k, :],
                                    start=(k == 0), stop=(k == K - 1))
                ins.then_inc(pe_unit, 1)
                if m == 0:
                    pe.wait_ge(block_ready, c + 1)
                    if i >= 1:
                        pe.wait_ge(colb_ready, i)
                    pe.matmul(colp[:, :], ones[:, :], csum[:, n, :], start=True, stop=True)\
                        .then_inc(col_ready, 1)

            for s in range(SLOTS):
                if s in UNIT_AT:
                    unit(UNIT_AT[s])
                if s - 2 in TILE_AT:
                    transpose_a(TILE_AT[s - 2])

            def three(out_, lh, ll, rh, rl, first, final):
                pe.matmul(out_, lh, rh, start=first, stop=False)
                pe.matmul(out_, lh, rl, start=False, stop=False)
                return pe.matmul(out_, ll, rh, start=False, stop=final)

            def transpose_h(g, k):
                if k == 0:
                    pe.wait_ge(xn_ready, g + 1)
                if not (isinstance(g, int) and k < 2):
                    pe.wait_ge(hl_ready, g * K + (k - 1))
                for m in range(M):
                    ins = pe.transpose(tpb[k % 2][:, m * P:(m + 1) * P], xg[0][:, m, k * P:(k + 1) * P],
                                       idf[:, :])
                ins.then_inc(t_ready, 1)

            def tok(m):
                return slice(m * P, (m + 1) * P)

            def ar_slice(g, k):
                if k == 0:
                    pe.wait_ge(wl_ready, RING)
                pe.wait_ge(hl_ready, g * K + (k + 1))
                for m in range(M):
                    if k == 0:
                        if isinstance(g, int):
                            pe.wait_ge(x1_ready, M * (ITS - 1) + m + 1)
                        elif m > 0:
                            pe.wait_ge(out_ready, g * ITS + (m + 1 - M))
                    both = arw[:, k, :, :].rearrange("p s n -> p (s n)")
                    pe.matmul(acc[m][:, 0:2 * AR], hh[:, k, tok(m)], both, start=(k == 0), stop=False)
                    ins = pe.matmul(acc[m][:, 0:2 * AR], hl[:, k, tok(m)], both, start=False,
                                    stop=(k == K - 1))
                    if k == K - 1:
                        ins.then_inc(ar_done, 1)

            transpose_h(0, 0)
            transpose_h(0, 1)
            for k in range(K):
                ar_slice(0, k)
                if k + 2 < K:
                    transpose_h(0, k + 2)

            def group(g, last):
                for j in range(NB):
                    for q in range(WP):
                        X = WP * j + q
                        s = X % RING
                        pe.wait_ge(wl_ready, g * WG + (LEAD + X + 1))
                        for kk in range(WK):
                            k = WK * q + kk
                            cols = slice(kk * NW, (kk + 1) * NW)
                            for m in range(M):
                                if k == 0 and j == 0:
                                    pe.wait_ge(ar_evac, g * M + (m + 1))
                                elif k == 0 and m > 0:
                                    pe.wait_ge(out_ready, g * ITS + (M * (j - 1) + m + 1))
                                elif k == 0 and j > 1:
                                    pe.wait_ge(out_ready, g * ITS + (M * (j - 2) + 1))
                                ins = three(bank(j, m)[:, :], hh[:, k, tok(m)], hl[:, k, tok(m)],
                                            wh[s][:, cols], wl[s][:, cols], k == 0, False)
                            if kk == WK - 1:
                                ins.then_inc(w_used, 1)
                            if j == NB - 1 and not last:
                                transpose_h(g + 1, k)
                        if j == 0 and q == 3:
                            pe.wait_ge(mids_ready, g + 1)
                            for m in range(M):
                                ins = pe.transpose(colp[:, tok(m)],
                                                   mids[:, m, :, :].rearrange("p e r -> p (e r)"), idf[:, :])
                            ins.then_inc(mt_ready, 1)
                    cols = slice(j * NW, (j + 1) * NW)
                    if j == 0:
                        pe.wait_ge(mtl_ready, g + 1)
                    for m in range(M):
                        three(bank(j, m)[:, :], mth[:, tok(m)], mtl[:, tok(m)], bh[:, cols], bl[:, cols],
                              False, True).then_inc(acc_done, 1)
                if not last:
                    for k in range(K):
                        ar_slice(g + 1, k)

            with pe.Fori(0, G - 1) as g:
                group(g, False)
            group(G - 1, True)


def kernel(x, ctx_4096, g_xattn, g_ffn, L0_xattn_x1_scale, L0_xattn_x1_zp, L0_xattn_x2_scale,
           L0_xattn_x2_zp, L0_ffn_base_W, L0_ffn_router_W, L0_ffn_lora_A, L0_ffn_lora_B):
    import numpy as np
    import concourse.bacc as bacc
    from concourse.bass_utils import run_bass_kernel_spmd

    scal = [L0_xattn_x1_scale, L0_xattn_x1_zp, L0_xattn_x2_scale, L0_xattn_x2_zp, g_xattn, g_ffn]
    lora_a = np.transpose(np.asarray(L0_ffn_lora_A), (1, 0, 2)).reshape(D, ER)
    arrays = {
        "in_x": np.asarray(x).reshape(TOK, D),
        "in_ctx": np.asarray(ctx_4096),
        "in_wt": np.asarray(L0_ffn_base_W).T,
        "in_ar": np.concatenate([lora_a, np.asarray(L0_ffn_router_W).T], axis=1),
        "in_lb": np.asarray(L0_ffn_lora_B).reshape(ER, D),
        "in_scal": np.broadcast_to(np.concatenate([np.asarray(s).reshape(1) for s in scal])[None, :], (P, 6)),
    }
    arrays = {n: np.ascontiguousarray(a) for n, a in arrays.items()}
    nc = bacc.Bacc("TRN2", target_bir_lowering=False, num_devices=1, dynamic_dma_scratch_size=4096)
    args = [nc.dram_tensor(n, a.shape, F32, kind="ExternalInput").ap() for n, a in arrays.items()]
    args.append(nc.dram_tensor("x1_scratch", (TOK, D), F32, kind="Internal").ap())
    args.append(nc.dram_tensor("out_0", (TOK, D), F32, kind="ExternalOutput").ap())
    build(nc, *args)
    r = run_bass_kernel_spmd(nc, [arrays], core_ids=[0])
    return r.results[0]["out_0"].reshape(np.asarray(x).shape)
```

```python
import concourse.bass as bass
from concourse import mybir
from contextlib import ExitStack

F32 = mybir.dt.float32
F32R = mybir.dt.float32r
BF16 = mybir.dt.bfloat16
F16 = mybir.dt.float16
U8 = mybir.dt.uint8
ALU = mybir.AluOpType
ACT = mybir.ActivationFunctionType
AX = mybir.AxisListType

P = 128
D = 2048
TOK = 2048
K = D // P
NW = 512
NB = D // NW
GT = 512
G = TOK // GT
M = GT // P
TILES = G * M
ITS = G * NB
E, R = 8, 16
ER = E * R
AR = ER + E
TOP_K = 2
SCALING = 2.0
EPS = 1e-5
MID = 128.0
PE_TILES = 4
PK = 4
CP = K // PK
CS = 3
WK = 2
WP = K // WK
WG = NB * WP
RING = 4
LEAD = 2 * RING
CHAIN_B = 58
KIB = 1024

UNIT_SLOT = [61, 69, 70, 76, 94, 96, 119, 135, 137, 138, 147, 164, 181, 191, 194, 200, 203, 237, 250, 264,
             281, 282, 303, 316, 322, 326, 333, 339, 343, 358, 364, 365, 433, 444, 466, 468, 469, 481, 495,
             507, 508, 514, 519, 548, 575, 576, 601, 615, 621, 644, 657, 677, 692, 720, 726, 732, 734, 738,
             761, 776, 807, 816, 836, 849]
TILE_SLOT = [0, 15, 29, 46, 58, 93, 145, 202, 289, 319, 338, 368, 497, 519, 539, 579]
PIECE_SLOT = [0, 24, 33, 38, 54, 60, 68, 75, 83, 95, 99, 104, 110, 136, 151, 161, 277, 278, 281, 327, 335,
              338, 352, 360, 362, 392, 413, 445, 482, 488, 525, 526]
COL_SLOT = [77, 120, 174, 192, 256, 286, 303, 345, 417, 467, 498, 577, 637, 657, 702, 795]
AFTER = dict(scale=12, quantise=10, widen=24, transpose=16, copy_aT=28, row_term=36,
             sums=34, col_term=24, add_col=35, evac=26, store=60)
UNIT_AT, TILE_AT, PIECE_AT, COL_AT = ({slot: i for i, slot in enumerate(table)}
                                      for table in (UNIT_SLOT, TILE_SLOT, PIECE_SLOT, COL_SLOT))
SLOTS = max(UNIT_AT) + max(AFTER.values()) + 1
B0 = 755
W_AT = {6: 0, 8: 1, 10: 2, 12: 3}


class Chain:

    def __init__(self, eng, sem, base=0):
        self.eng, self.sem, self.base, self.n = eng, sem, base, 0

    def __call__(self, ins, wait=True):
        self.n += 1
        ins.then_inc(self.sem, 1)
        if wait:
            self.eng.wait_ge(self.sem, self.base + self.n)


def build(nc, x, ctx, wt, ar, lb, scal, x1s, out):
    es = ExitStack()
    with es:
        top = nc.sbuf_base

        def at(name, off, shape, dt):
            return nc.alloc_sbuf_tensor_at(name, shape, dt, offset=off)

        def psum(name, shape, dt):
            return es.enter_context(nc.psum_tensor(name, shape, dt))

        def sem(name):
            return es.enter_context(nc.semaphore(name))

        XG0 = (top + 31) // 32 * 32
        XG1 = XG0 + 32 * KIB
        AT0 = XG1 + 32 * KIB
        AT1 = AT0 + 16 * KIB
        CTX = AT1 + 16 * KIB
        CST = CTX + 64 * KIB
        SMALL = CST + 28 * KIB
        LAST = SMALL + 22 * KIB
        xg = [at("x_group_even", XG0, [P, M, D], F32), at("x_group_odd", XG1, [P, M, D], F32)]
        aT = [at("aT_even", AT0, [P, K, GT], BF16), at("aT_odd", AT1, [P, K, GT], BF16)]
        ctxq = at("ctx_quant", CTX, [P, NB, K, NW], BF16)
        cst = [at(f"ctx_stage{s}", CST + 8 * KIB * s, [P, PK, NW], F32) for s in range(CS)]
        cu8 = [at(f"ctx_u8_{s}", CST + 24 * KIB + 2 * KIB * s, [P, PK, NW], U8) for s in range(2)]
        anat = at("a_rows", SMALL, [P, D], BF16)
        xu8 = at("x_u8", SMALL + 4 * KIB, [P, D], U8)
        csum = at("ctx_part_sums", SMALL + 6 * KIB, [P, NB, NW], F16)
        tree = at("ctx_tree_sums", SMALL + 10 * KIB, [P, K // 2, NW], F16)
        colb = [at(f"col_term{s}", SMALL + 18 * KIB + 2 * KIB * s, [P, NW], F32) for s in range(2)]
        wst = [at(f"w_stage{s}", AT0 + 4 * KIB * s, [P, WK * NW], F32) for s in range(RING)]
        wh = [at(f"w_hi{s}", XG1 + 8 * KIB * s, [P, WK * NW], F32R) for s in range(RING)]
        wl = [at(f"w_lo{s}", XG1 + 8 * KIB * s + 4 * KIB, [P, WK * NW], F32R) for s in range(RING)]
        hh = at("hT_hi", CTX, [P, K, GT], F32R)
        hl = at("hT_lo", CTX + 32 * KIB, [P, K, GT], F32R)
        arw = at("ar_hi_lo", CST, [P, K, 2, AR], F32R)
        bh = at("b_hi", AT1, [P, D], F32R)
        bl = at("b_lo", AT1 + 8 * KIB, [P, D], F32R)
        res = [at(f"residual{m}", SMALL + 2 * KIB * m, [P, NW], F32) for m in range(M)]
        mids = at("mid_scaled", SMALL + 8 * KIB, [P, M, E, R], F32)
        mth = at("midT_hi", SMALL + 10 * KIB, [P, GT], F32R)
        mtl = at("midT_lo", SMALL + 12 * KIB, [P, GT], F32R)
        mid = at("mid", SMALL + 14 * KIB, [P, M, AR], F32)
        rank = at("router_rank", SMALL + 17 * KIB, [P, M, E, E], F32)
        rankeq = at("router_rank_eq", SMALL + 18 * KIB, [P, M, E, E], F32)
        o = [LAST]

        def keep(name, shape, dt, size):
            off, o[0] = o[0], o[0] + (size + 31) // 32 * 32
            return at(name, off, shape, dt)

        idf = keep("identity_f32", [P, P], F32, 512)
        idb = keep("identity_bf16", [P, P], BF16, 256)
        ones = keep("ones_f16", [P, P], F16, 256)
        tri = keep("earlier_expert", [P, E, E], F32, 256)
        sc = keep("scalars", [P, 6], F32, 24)
        th = keep("gates", [P, 2], F32, 8)
        cst_ = keep("constants", [P, 8], F32, 32)
        st = keep("bn_chunks", [P, 4 * 6], F32, 96)
        st2 = keep("bn_chunks_group", [P, M, 4 * 6], F32, 384)
        mv = keep("mean_var", [P, M, 2], F32, 32)
        ve = keep("var_eps", [P, M], F32, 16)
        sd = keep("std", [P, M], F32, 16)
        rs = keep("rstd", [P, M], F32, 16)
        nt = keep("newton", [P, M], F32, 16)
        xmv = keep("x_mean_var", [P, TILES, 2], F32, 8 * TILES)
        xve = keep("x_var_eps", [P, TILES], F32, 4 * TILES)
        xsd = keep("x_std", [P, TILES], F32, 4 * TILES)
        xrs = keep("x_rstd", [P, 1], F32, 4)
        qs = keep("quant_scale_bias", [P, TILES, 2], F32, 8 * TILES)
        spare = keep("spare", [P, 1], F32, 4)
        asum = keep("a_row_sum", [P, 1], F32, 4)
        crow = keep("row_terms", [P, TILES], F32, 64)
        lg = keep("logits_minus_max", [P, M, E], F32, 128)
        ex = keep("exp_logits", [P, M, E], F32, 128)
        rk = keep("rank", [P, M, E], F32, 128)
        wsel = keep("expert_weights", [P, M, E], F32, 128)
        mx = keep("logit_max", [P, M], F32, 16)
        den = keep("weight_sum", [P, M], F32, 16)
        assert o[0] <= nc.sbuf_usable_end, (o[0], nc.sbuf_usable_end)

        s1, z1, s2, z2 = (sc[:, i:i + 1] for i in range(4))
        inv1, inv2, cg, d1, d2, cd1, cd2, ckd = (cst_[:, i:i + 1] for i in range(8))
        gate2 = th[:, 1:2]

        acc = [psum(f"acc{m}", [P, NW], F32) for m in range(M)]
        tpa = psum("aT_psum", [P, K, P], BF16)
        tpb = [tpa[:, 8 * s:8 * s + 8, :].rearrange("p a b -> p (a b)").bitcast(F32) for s in range(2)]
        colp = psum("col_psum", [P, NW], F32)
        acc0b = psum("acc0_even", [P, NW], F32)

        def bank(j, m):
            return acc0b if m == 0 and j % 2 == 0 else acc[m]

        arp = [acc[0], colp, tpb[0], tpb[1]]
        th0 = [acc0b, acc[1], acc[2]]

        s_const = sem("s_const")
        s_gate = sem("s_gate")
        s_cst = sem("s_cst")
        s_id = sem("s_id")
        s_chain = sem("s_chain")
        x_in = [[sem(f"x_in{a}{m}") for m in range(M)] for a in range(2)]
        var_ready = sem("var_ready")
        std_ready = sem("std_ready")
        qs_ready = sem("qs_ready")
        xu8_ready = sem("xu8_ready")
        a_ready = sem("a_ready")
        tp_ready = sem("tp_ready")
        aT_ready = sem("aT_ready")
        aT_moved = sem("aT_moved")
        xr_ready = sem("xr_ready")
        c_in = [sem(f"c_in{s}") for s in range(CS)]
        cu8_ready = sem("cu8_ready")
        c_conv = sem("c_conv")
        block_ready = sem("block_ready")
        col_ready = sem("col_ready")
        colb_ready = sem("colb_ready")
        x1_ready = sem("x1_ready")
        pe_unit = sem("pe_unit")
        bank_read = sem("bank_read")
        x1_stored = [sem(f"x1_stored{a}") for a in range(2)]
        s_chain_b = sem("s_chain_b")
        g_in = [sem(f"g_in{m}") for m in range(M)]
        xn_ready = sem("xn_ready")
        var2_ready = sem("var2_ready")
        std2_ready = sem("std2_ready")
        w_in = [sem(f"w_in{s}") for s in range(RING)]
        wh_ready = sem("wh_ready")
        wl_ready = sem("wl_ready")
        w_used = sem("w_used")
        t_ready = sem("t_ready")
        hh_ready = sem("hh_ready")
        hl_ready = sem("hl_ready")
        ar_done = sem("ar_done")
        lg_ready = sem("lg_ready")
        ex_ready = sem("ex_ready")
        mids_ready = sem("mids_ready")
        mt_ready = sem("mt_ready")
        mth_ready = sem("mth_ready")
        mtl_ready = sem("mtl_ready")
        acc_done = sem("acc_done")
        r_in = [sem(f"r_in{m}") for m in range(M)]
        out_ready = sem("out_ready")
        out_stored = [sem(f"out_stored{m}") for m in range(M)]

        def h_psum(g, k):
            return th0[k % 3][:, :] if isinstance(g, int) else tpb[k % 2]

        def rows(t, g, m, n):
            return t[bass.ds(g * GT + m * P, P), n * NW:(n + 1) * NW]

        def w_piece(X):
            Y = X % WG
            k0, n = WK * (Y % WP), Y // WP
            return wt[k0 * P:(k0 + WK) * P, n * NW:(n + 1) * NW].rearrange("(k p) n -> p k n", p=P)

        def lead_piece(i):
            return 4 * AR if i < RING else NW

        block = es.enter_context(nc.Block())

        @block.sync
        def _(sp):
            def load_x(t):
                g, m = t // M, t % M
                if g >= 2:
                    sp.wait_ge(x1_stored[g % 2], 16 * NB * (g // 2))
                sp.dma_start(xg[g % 2][:, m, :], x[t * P:(t + 1) * P, :]).then_inc(x_in[g % 2][m], 16)

            def load_ctx(q):
                c, p = q // CP, q % CP
                b, n = c // NB, c % NB
                if q >= CS:
                    sp.wait_ge(cu8_ready, q - CS + 1)
                src = ctx[b, p * PK * P:(p + 1) * PK * P, n * NW:(n + 1) * NW]
                sp.dma_start(cst[q % CS][:, :, :], src.rearrange("(k p) n -> p k n", p=P))\
                    .then_inc(c_in[q % CS], 16)

            def load_group(g):
                for m in range(M):
                    sp.dma_start(xg[0][:, m, :], x1s[bass.ds(g * GT + m * P, P), :])\
                        .then_inc(g_in[m], 16)

            def load_lead(i, slot):
                w = lead_piece(i)
                if i < RING:
                    src = ar[4 * i * P:4 * (i + 1) * P, :].rearrange("(k p) n -> p k n", p=P)
                    dst = wst[slot][:, 0:w].rearrange("p (k n) -> p k n", n=AR)
                else:
                    src, dst = lb[:, (i - RING) * NW:(i - RING + 1) * NW], wst[slot][:, 0:w]
                sp.dma_start(dst, src).then_inc(w_in[slot], 16)

            def load_w(X):
                sp.dma_start(wst[X % RING][:, :].rearrange("p (k n) -> p k n", n=NW), w_piece(X))\
                    .then_inc(w_in[X % RING], 16)

            def load_res(g, n):
                for m in range(M):
                    sp.dma_start(res[m][:, :], rows(x1s, g, m, n)).then_inc(r_in[m], 16)

            sp.dma_start(sc[:, :], scal).then_inc(s_const, 16)
            load_x(0)
            load_ctx(0)
            for s in range(1, SLOTS):
                if s in PIECE_AT:
                    load_ctx(PIECE_AT[s])
                if s in TILE_AT:
                    load_x(TILE_AT[s])
                if s == B0:
                    sp.wait_ge(x1_stored[0], 16 * NB * 2)
                    load_group(0)
                    sp.wait_ge(pe_unit, M * NB * (G - 1))
                    for r in range(RING):
                        load_lead(r, r)
            for X in range(RING):
                sp.wait_ge(wl_ready, X + 1)
                load_w(X)
            for a in range(2):
                sp.wait_ge(x1_stored[a], 16 * NB * 2)
            load_res(0, 0)
            for r in range(RING):
                sp.wait_ge(wl_ready, RING + r + 1)
                load_lead(RING + r, r)

            def group(g, last):
                for j in range(NB):
                    for q in range(WP):
                        X = WP * j + RING + q
                        if not (last and X >= WG):
                            sp.wait_ge(wl_ready, g * WG + (LEAD + X - RING + 1))
                            load_w(X)
                        if j == 0 and q == 0 and not last:
                            sp.wait_ge(t_ready, g * K + K)
                            load_group(g + 1)
                    if not (last and j == NB - 1):
                        for m in range(M):
                            sp.wait_ge(out_stored[m], g * (16 * NB) + 16 * (j + 1))
                        if j < NB - 1:
                            load_res(g, j + 1)
                        else:
                            load_res(g + 1, 0)

            with sp.Fori(0, G - 1) as g:
                group(g, False)
            group(G - 1, True)
            for m in range(M):
                sp.wait_ge(out_stored[m], 16 * ITS)

        @block.gpsimd
        def _(pool):
            pool.memset(idf[:, :], 0.0).then_inc(s_id, 1)
            pool.memset(idb[:, :], 0.0).then_inc(s_id, 1)
            pool.memset(ones[:, :], 1.0).then_inc(s_id, 1)
            pool.memset(tri[:, :, :], 1.0).then_inc(s_id, 1)
            pool.wait_ge(s_id, 4)
            for t in (idf, idb):
                pool.affine_select(out=t[:, :], in_=t[:, :], compare_op=ALU.not_equal, fill=1.0, base=0,
                                   pattern=[[-1, P]], channel_multiplier=1).then_inc(s_id, 1)
            pool.affine_select(out=tri[:, :, :], in_=tri[:, :, :], compare_op=ALU.is_gt, fill=0.0, base=0,
                               pattern=[[1, E], [-1, E]], channel_multiplier=0).then_inc(s_id, 1)

            def ctx_widen(q):
                c, p = q // CP, q % CP
                pool.wait_ge(cu8_ready, q + 1)
                if c >= NB:
                    pool.wait_ge(pe_unit, M * (c + 1))
                pool.tensor_scalar(ctxq[:, c % NB, PK * p:PK * (p + 1), :], cu8[q % 2][:, :, :], -MID, 1.0,
                                   ALU.add, ALU.mult).then_inc(c_conv, 1)

            def row_term(t):
                pool.wait_ge(a_ready, t + 1)
                tile = xg[(t // M) % 2][:, t % M, :]
                pool.tensor_scalar(tile, tile, crow[:, t:t + 1], 1.0, ALU.add, ALU.mult).then_inc(xr_ready, 1)

            def add_col_term(u):
                i, m = u // M, u % M
                g, n = i // NB, i % NB
                pool.wait_ge(colb_ready, i + 1)
                pool.wait_ge(bank_read, u + 1)
                blk = xg[g % 2][:, m, n * NW:(n + 1) * NW]
                pool.tensor_tensor(blk, blk, colb[i % 2][:, :], ALU.add).then_inc(x1_ready, 1)

            for s in range(SLOTS):
                if s - AFTER["row_term"] in TILE_AT:
                    row_term(TILE_AT[s - AFTER["row_term"]])
                if s - AFTER["add_col"] in UNIT_AT:
                    add_col_term(UNIT_AT[s - AFTER["add_col"]])
                if s in PIECE_AT:
                    ctx_widen(PIECE_AT[s])

        @block.scalar
        def _(act):
            act.wait_ge(s_const, 16)
            act.activation(th[:, :], sc[:, 4:6], ACT.Tanh).then_inc(s_gate, 1)
            act.activation(spare[:, :], s1, ACT.Sqrt)

            def std(t):
                act.wait_ge(var_ready, t + 1)
                act.activation(xsd[:, t:t + 1], xve[:, t:t + 1], ACT.Sqrt).then_inc(std_ready, 1)

            def x_to_u8(t):
                act.wait_ge(qs_ready, t + 1)
                if t >= 1:
                    act.wait_ge(a_ready, t)
                act.activation(xu8[:, :], xg[(t // M) % 2][:, t % M, :], ACT.Identity,
                               scale=qs[:, t, 0:1], bias=qs[:, t, 1:2]).then_inc(xu8_ready, 1)

            def ctx_to_u8(q):
                act.wait_ge(c_in[q % CS], 16 * (q // CS + 1))
                if q >= 2:
                    act.wait_ge(c_conv, q - 1)
                act.activation(cu8[q % 2][:, :, :], cst[q % CS][:, :, :], ACT.Identity,
                               scale=inv2, bias=z2).then_inc(cu8_ready, 1)

            def aT_copy(t):
                g, m = t // M, t % M
                dst = aT[g % 2][:, :, m * P:(m + 1) * P]
                if g >= 2:
                    act.wait_ge(pe_unit, M * NB * (g - 1))
                if t < PE_TILES:
                    act.wait_ge(tp_ready, t + 1)
                    act.activation(dst, tpa[:, :, :], ACT.Copy).then_inc(aT_ready, 1)
                else:
                    act.wait_ge(a_ready, t + 1)
                    act.dma_start_transpose(dst, anat[:, :]).then_inc(aT_moved, 16)

            def store_x1(i):
                g, n = i // NB, i % NB
                act.wait_ge(x1_ready, M * (i + 1))
                dst = x1s[g * GT:(g + 1) * GT, n * NW:(n + 1) * NW].rearrange("(m p) n -> p m n", p=P)
                act.dma_start(dst, xg[g % 2][:, :, n * NW:(n + 1) * NW]).then_inc(x1_stored[g % 2], 16)

            act.wait_ge(s_cst, 1)
            for s in range(SLOTS):
                if UNIT_AT.get(s - AFTER["store"], 0) in range(M - 1, M * (ITS - 1), M):
                    store_x1(UNIT_AT[s - AFTER["store"]] // M)
                if s in TILE_AT:
                    std(TILE_AT[s])
                if s in PIECE_AT:
                    ctx_to_u8(PIECE_AT[s])
                if s - AFTER["copy_aT"] in TILE_AT:
                    aT_copy(TILE_AT[s - AFTER["copy_aT"]])
                if s - AFTER["quantise"] in TILE_AT:
                    x_to_u8(TILE_AT[s - AFTER["quantise"]])
                if s == B0 + M:
                    act.wait_ge(var2_ready, 1)
                    act.activation(sd[:, :], ve[:, :], ACT.Sqrt).then_inc(std2_ready, 1)
                if s == B0 + M + 2:
                    for r in range(RING):
                        act.wait_ge(w_in[r], 16)
                        w = lead_piece(r)
                        act.activation(arw[:, 4 * r:4 * r + 4, 0, :],
                                       wst[r][:, 0:w].rearrange("p (k n) -> p k n", n=AR), ACT.Copy)\
                            .then_inc(wh_ready, 1)

            def w_hi(g, X, lead=LEAD):
                s = X % RING
                act.wait_ge(w_in[s], g * (16 * WG // RING) + 16 * ((lead + X) // RING + 1))
                if lead == LEAD:
                    act.wait_ge(w_used, g * WG + (X - RING + 1))
                act.activation(wh[s][:, :], wst[s][:, :], ACT.Copy).then_inc(wh_ready, 1)

            def b_hi(r):
                act.wait_ge(w_in[r], 16 * 3)
                act.activation(bh[:, r * NW:(r + 1) * NW], wst[r][:, 0:NW], ACT.Copy).then_inc(wh_ready, 1)

            def h_hi(g, k):
                act.wait_ge(t_ready, g * K + (k + 1))
                act.activation(hh[:, k, :], h_psum(g, k), ACT.Copy).then_inc(hh_ready, 1)

            for k in range(K):
                h_hi(0, k)
                if k == 1:
                    store_x1(ITS - 1)
                if k in W_AT:
                    if W_AT[k] == 0:
                        act.wait_ge(x1_stored[1], 16 * NB * 2)
                    w_hi(0, W_AT[k], lead=RING)
            for i in range(RING):
                b_hi(i)

            def group(g, last):
                act.wait_ge(lg_ready, g + 1)
                act.activation(ex[:, :, :], lg[:, :, :], ACT.Exp).then_inc(ex_ready, 1)
                for j in range(NB):
                    for q in range(WP):
                        if j == 0 and q == 3:
                            act.wait_ge(mt_ready, g + 1)
                            act.activation(mth[:, :], colp[:, :], ACT.Copy).then_inc(mth_ready, 1)
                        if j == 1 and q == 4 and not last:
                            act.wait_ge(var2_ready, g + 2)
                            act.activation(sd[:, :], ve[:, :], ACT.Sqrt).then_inc(std2_ready, 1)
                        if j == NB - 1 and not last:
                            h_hi(g + 1, 2 * q)
                            h_hi(g + 1, 2 * q + 1)
                        X = WP * j + RING + q
                        if not (last and X >= WG):
                            w_hi(g, X)
                    for m in range(M):
                        act.wait_ge(out_ready, g * ITS + (M * j + m + 1))
                        act.dma_start(rows(out, g, m, j), res[m][:, :]).then_inc(out_stored[m], 16)

            with act.Fori(0, G - 1) as g:
                group(g, False)
            group(G - 1, True)

        @block.vector
        def _(dve):
            link = Chain(dve, s_chain)
            dve.wait_ge(s_const, 16)
            link(dve.reciprocal(inv1, s1))
            link(dve.reciprocal(inv2, s2))
            link(dve.tensor_scalar(d1, z1, -1.0, MID, ALU.mult, ALU.add))
            link(dve.tensor_scalar(d2, z2, -1.0, MID, ALU.mult, ALU.add))
            dve.wait_ge(s_gate, 1)
            link(dve.tensor_scalar(cg, th[:, 0:1], s1, s2, ALU.mult, ALU.mult))
            link(dve.tensor_scalar(cd1, cg, d1, None, ALU.mult))
            link(dve.tensor_scalar(cd2, cg, d2, None, ALU.mult))
            dve.tensor_scalar(ckd, cd1, d2, float(D), ALU.mult, ALU.mult).then_inc(s_cst, 1)
            dve.wait_ge(s_cst, 1)

            def chunk_stats(chain, chunks, src):
                for c in range(D // NW):
                    chain(dve.bn_stats(chunks[:, 6 * c:6 * c + 6], src[:, c * NW:(c + 1) * NW]), wait=c == D // NW - 1)

            def rstd(chain, v, root, y):
                n = nt[:, 0:v.shape[1]]
                chain(dve.reciprocal(y, root))
                if v.shape[1] == 1:
                    chain(dve.scalar_tensor_tensor(out=n, in0=y, scalar=y, in1=v, op0=ALU.mult, op1=ALU.mult))
                else:
                    chain(dve.tensor_tensor(n, y, y, ALU.mult))
                    chain(dve.tensor_tensor(n, n, v, ALU.mult))
                chain(dve.tensor_scalar(n, n, -0.5, 1.5, ALU.mult, ALU.add))
                chain(dve.tensor_tensor(y, y, n, ALU.mult))

            def x_stats(t):
                g, m = t // M, t % M
                dve.wait_ge(x_in[g % 2][m], 16 * (g // 2 + 1))
                chunk_stats(link, st[:, :], xg[g % 2][:, m, :])
                link(dve.bn_aggr(xmv[:, t, :], st[:, :]))
                dve.tensor_scalar(xve[:, t:t + 1], xmv[:, t, 1:2], EPS, None, ALU.add).then_inc(var_ready, 1)

            def x_scale(t):
                dve.wait_ge(std_ready, t + 1)
                rstd(link, xve[:, t:t + 1], xsd[:, t:t + 1], xrs[:, :])
                link(dve.tensor_scalar(qs[:, t, 0:1], xrs[:, :], inv1, None, ALU.mult))
                dve.scalar_tensor_tensor(out=qs[:, t, 1:2], in0=xmv[:, t, 0:1], scalar=qs[:, t, 0:1], in1=z1,
                                         op0=ALU.mult, op1=ALU.subtract, reverse1=True).then_inc(qs_ready, 1)

            def x_widen(t):
                dve.wait_ge(xu8_ready, t + 1)
                if t >= 1:
                    if t <= PE_TILES:
                        dve.wait_ge(tp_ready, t)
                    else:
                        dve.wait_ge(aT_moved, 16 * (t - PE_TILES))
                link(dve.tensor_scalar(anat[:, :], xu8[:, :], -MID, 0.0, ALU.add, ALU.add,
                                       accum_out=asum[:, :]))
                dve.tensor_scalar(crow[:, t:t + 1], asum[:, :], cd2, ckd, ALU.mult, ALU.add)\
                    .then_inc(a_ready, 1)

            def ctx_sums(c):
                dve.wait_ge(c_conv, CP * (c + 1))
                if c >= 1:
                    dve.wait_ge(block_ready, c)
                if c >= NB:
                    dve.wait_ge(col_ready, c + 1)
                src, w = ctxq[:, c % NB, :, :], K // 2
                while w:
                    dst = tree[:, 0:w, :] if w > 1 else csum[:, c % NB, :].unsqueeze(1)
                    ins = dve.tensor_tensor(dst, src[:, 0:w, :], src[:, w:2 * w, :], ALU.add)
                    if w > 1:
                        link(ins)
                    else:
                        ins.then_inc(block_ready, 1)
                    src, w = tree, w // 2

            def col_term(i):
                dve.wait_ge(col_ready, i + 1)
                if i >= 2:
                    dve.wait_ge(x1_ready, M * (i - 1))
                dve.tensor_scalar(colb[i % 2][:, :], colp[:, :], cd1, None, ALU.mult)\
                    .then_inc(colb_ready, 1)

            def evac(u):
                i, m = u // M, u % M
                g, n = i // NB, i % NB
                dve.wait_ge(pe_unit, u + 1)
                dve.wait_ge(xr_ready, M * g + m + 1)
                blk = xg[g % 2][:, m, n * NW:(n + 1) * NW]
                dve.scalar_tensor_tensor(out=blk, in0=acc[m][:, :], scalar=cg, in1=blk, op0=ALU.mult,
                                         op1=ALU.add).then_inc(bank_read, 1)

            def group_stats(chain, g, m):
                dve.wait_ge(g_in[m], g * 16 + 16)
                chunk_stats(chain, st2[:, m, :], xg[0][:, m, :])

            def group_mean_var(chain, m):
                chain(dve.bn_aggr(mv[:, m, :], st2[:, m, :]))

            def group_var(chain):
                dve.tensor_scalar(ve[:, :], mv[:, :, 1], EPS, None, ALU.add).then_inc(var2_ready, 1)

            def normalise(chain, m):
                blk = xg[0][:, m, :]
                ins = dve.tensor_scalar(blk, blk, mv[:, m, 0:1], rs[:, m:m + 1], ALU.subtract, ALU.mult)
                if m == M - 1:
                    ins.then_inc(xn_ready, 1)
                else:
                    chain(ins)

            for s in range(SLOTS):
                if s - AFTER["widen"] in TILE_AT:
                    x_widen(TILE_AT[s - AFTER["widen"]])
                if s - AFTER["scale"] in TILE_AT:
                    x_scale(TILE_AT[s - AFTER["scale"]])
                if PIECE_AT.get(s - AFTER["sums"], 0) % CP == CP - 1:
                    ctx_sums(PIECE_AT[s - AFTER["sums"]] // CP)
                if s in TILE_AT:
                    x_stats(TILE_AT[s])
                if s - AFTER["evac"] in UNIT_AT:
                    evac(UNIT_AT[s - AFTER["evac"]])
                if s - AFTER["col_term"] in COL_AT:
                    col_term(COL_AT[s - AFTER["col_term"]])
                if B0 + 1 <= s <= B0 + M:
                    group_stats(link, 0, s - B0 - 1)
                    group_mean_var(link, s - B0 - 1)
                if s == B0 + M:
                    group_var(link)
                if s == B0 + M + 1:
                    dve.wait_ge(std2_ready, 1)
                    rstd(link, ve[:, :], sd[:, :], rs[:, :])
                if B0 + M + 1 <= s <= B0 + 2 * M:
                    normalise(link, s - B0 - M - 1)
                if s == B0 + 2 * M + 1:
                    for r in range(RING):
                        dve.wait_ge(wh_ready, r + 1)
                        w = lead_piece(r)
                        dve.tensor_tensor(arw[:, 4 * r:4 * r + 4, 1, :],
                                          wst[r][:, 0:w].rearrange("p (k n) -> p k n", n=AR),
                                          arw[:, 4 * r:4 * r + 4, 0, :].bitcast(F32), ALU.subtract)\
                            .then_inc(wl_ready, 1)

            def w_lo(g, X, lead=LEAD):
                s = X % RING
                dve.wait_ge(wh_ready, g * WG + (lead + X + 1))
                dve.tensor_tensor(wl[s][:, :], wst[s][:, :], wh[s][:, :].bitcast(F32), ALU.subtract)\
                    .then_inc(wl_ready, 1)

            def b_lo(r):
                dve.wait_ge(wh_ready, LEAD + r + 1)
                cols = slice(r * NW, (r + 1) * NW)
                dve.tensor_tensor(bl[:, cols], wst[r][:, 0:NW], bh[:, cols].bitcast(F32), ALU.subtract)\
                    .then_inc(wl_ready, 1)

            def h_lo(g, k):
                dve.wait_ge(hh_ready, g * K + (k + 1))
                dve.tensor_tensor(hl[:, k, :], h_psum(g, k), hh[:, k, :].bitcast(F32), ALU.subtract)\
                    .then_inc(hl_ready, 1)

            for k in range(K):
                h_lo(0, k)
                if k in W_AT:
                    w_lo(0, W_AT[k], lead=RING)
            for i in range(RING):
                b_lo(i)

            def router(chain, g):
                for m in range(M):
                    dve.wait_ge(ar_done, g * M + (m + 1))
                    chain(dve.tensor_copy(mid[:, m, :], arp[m][:, 0:AR]), wait=m == M - 1)
                for m in range(M):
                    chain(dve.tensor_tensor(mid[:, m, :], arp[m][:, AR:2 * AR], mid[:, m, :], ALU.add),
                          wait=m == M - 1)
                L = mid[:, :, ER:AR]
                chain(dve.tensor_reduce(mx[:, :], L, AX.X, ALU.max))
                dve.tensor_tensor(lg[:, :, :], L, mx[:, :].unsqueeze(2).to_broadcast([P, M, E]),
                                  ALU.subtract).then_inc(lg_ready, 1)
                for m in range(M):
                    lj = mid[:, m, ER:AR].unsqueeze(1).to_broadcast([P, E, E])
                    le = mid[:, m, ER:AR].unsqueeze(2).to_broadcast([P, E, E])
                    chain(dve.tensor_tensor(rank[:, m, :, :], lj, le, ALU.is_gt))
                    chain(dve.tensor_tensor(rankeq[:, m, :, :], lj, le, ALU.is_equal))
                    chain(dve.tensor_tensor(rankeq[:, m, :, :], rankeq[:, m, :, :], tri[:, :, :], ALU.mult))
                chain(dve.tensor_tensor(rank[:, :, :, :], rank[:, :, :, :], rankeq[:, :, :, :], ALU.add))
                chain(dve.tensor_reduce(rk[:, :, :], rank[:, :, :, :], AX.X, ALU.add))
                dve.wait_ge(ex_ready, g + 1)
                chain(dve.scalar_tensor_tensor(out=wsel[:, :, :], in0=rk[:, :, :], scalar=float(TOP_K),
                                               in1=ex[:, :, :], op0=ALU.is_lt, op1=ALU.mult))
                chain(dve.tensor_reduce(den[:, :], wsel[:, :, :], AX.X, ALU.add))
                chain(dve.reciprocal(den[:, :], den[:, :]))
                chain(dve.scalar_tensor_tensor(out=wsel[:, :, :], in0=wsel[:, :, :], scalar=SCALING,
                                               in1=den[:, :].unsqueeze(2).to_broadcast([P, M, E]),
                                               op0=ALU.mult, op1=ALU.mult))
                for m in range(M):
                    ins = dve.tensor_tensor(mids[:, m, :, :],
                                            mid[:, m, 0:ER].rearrange("p (e r) -> p e r", r=R),
                                            wsel[:, m, :].unsqueeze(2).to_broadcast([P, E, R]), ALU.mult)
                    if m == M - 1:
                        ins.then_inc(mids_ready, 1)
                    else:
                        chain(ins)

            def group(g, last):
                chain = Chain(dve, s_chain_b, g * CHAIN_B)
                router(chain, g)
                for j in range(NB):
                    for q in range(WP):
                        if j == 0 and q == 3:
                            dve.wait_ge(mth_ready, g + 1)
                            dve.tensor_tensor(mtl[:, :], colp[:, :], mth[:, :].bitcast(F32), ALU.subtract)\
                                .then_inc(mtl_ready, 1)
                        if not last and j == 1:
                            if q < M:
                                group_stats(chain, g + 1, q)
                            if q == M + 1:
                                dve.wait_ge(std2_ready, g + 2)
                                rstd(chain, ve[:, :], sd[:, :], rs[:, :])
                                for m in range(M):
                                    normalise(chain, m)
                        if j == NB - 1 and not last and q < WP - 1:
                            h_lo(g + 1, 2 * q)
                            h_lo(g + 1, 2 * q + 1)
                        X = WP * j + RING + q
                        if q < WP - 1 and not (last and X >= WG):
                            w_lo(g, X)
                        if not last and j == 1 and q < M:
                            group_mean_var(chain, q)
                            if q == M - 1:
                                group_var(chain)
                    for m in range(M):
                        if m == M - 1 and j == NB - 1 and not last:
                            h_lo(g + 1, K - 2)
                            h_lo(g + 1, K - 1)
                        dve.wait_ge(acc_done, g * ITS + (M * j + m + 1))
                        dve.wait_ge(r_in[m], g * (16 * NB) + 16 * (j + 1))
                        dve.scalar_tensor_tensor(out=res[m][:, :], in0=bank(j, m)[:, :], scalar=gate2,
                                                 in1=res[m][:, :], op0=ALU.mult, op1=ALU.add)\
                            .then_inc(out_ready, 1)
                    if not (last and j == NB - 1):
                        w_lo(g, WP * (j + 1) + RING - 1)
                assert last or chain.n == CHAIN_B, chain.n

            with dve.Fori(0, G - 1) as g:
                group(g, False)
            group(G - 1, True)

        @block.tensor
        def _(pe):
            pe.wait_ge(s_id, 7)

            def transpose_a(t):
                pe.wait_ge(a_ready, t + 1)
                if t >= 1:
                    pe.wait_ge(aT_ready, t)
                for k in range(K):
                    ins = pe.transpose(tpa[:, k, :], anat[:, k * P:(k + 1) * P], idb[:, :])
                ins.then_inc(tp_ready, 1)

            def unit(u):
                i, m = u // M, u % M
                g, n = i // NB, i % NB
                c = NB * (g // 2) + n
                pe.wait_ge(c_conv, CP * (c + 1))
                t = M * g + m
                if t < PE_TILES:
                    pe.wait_ge(aT_ready, t + 1)
                else:
                    pe.wait_ge(aT_moved, 16 * (t + 1 - PE_TILES))
                if i >= 1:
                    pe.wait_ge(bank_read, u - M + 1)
                for k in range(K):
                    ins = pe.matmul(acc[m][:, :], aT[g % 2][:, k, m * P:(m + 1) * P], ctxq[:, n, k, :],
                                    start=(k == 0), stop=(k == K - 1))
                ins.then_inc(pe_unit, 1)

            def col_sums(i):
                n = i % NB
                pe.wait_ge(block_ready, NB * (i // (2 * NB)) + n + 1)
                if i >= 1:
                    pe.wait_ge(colb_ready, i)
                pe.matmul(colp[:, :], ones[:, :], csum[:, n, :], start=True, stop=True)\
                    .then_inc(col_ready, 1)

            for s in range(SLOTS):
                if s in UNIT_AT:
                    unit(UNIT_AT[s])
                if s in COL_AT:
                    col_sums(COL_AT[s])
                if TILE_AT.get(s - AFTER["transpose"], TILES) < PE_TILES:
                    transpose_a(TILE_AT[s - AFTER["transpose"]])

            def three(out_, lh, ll, rh, rl, first, final):
                pe.matmul(out_, lh, rh, start=first, stop=False)
                pe.matmul(out_, lh, rl, start=False, stop=False)
                return pe.matmul(out_, ll, rh, start=False, stop=final)

            def transpose_h(g, k):
                if k == 0:
                    pe.wait_ge(xn_ready, g + 1)
                if not isinstance(g, int):
                    pe.wait_ge(hl_ready, g * K + (k - 1))
                elif k >= 3:
                    pe.wait_ge(hl_ready, k - 2)
                elif k >= 1:
                    pe.wait_ge(bank_read, M * (ITS - 1) + k + 1)
                for m in range(M):
                    ins = pe.transpose(h_psum(g, k)[:, m * P:(m + 1) * P], xg[0][:, m, k * P:(k + 1) * P],
                                       idf[:, :])
                ins.then_inc(t_ready, 1)

            def tok(m):
                return slice(m * P, (m + 1) * P)

            def ar_slice(g, k):
                if k == 0:
                    pe.wait_ge(wl_ready, RING)
                pe.wait_ge(hl_ready, g * K + (k + 1))
                for m in range(M):
                    if k == 0 and m == 0:
                        if isinstance(g, int):
                            pe.wait_ge(bank_read, M * (ITS - 1) + 1)
                        else:
                            pe.wait_ge(out_ready, g * ITS - (M - 1))
                    if k == 0 and m == 1 and isinstance(g, int):
                        pe.wait_ge(colb_ready, ITS)
                    if k == 0 and m >= 2 and not isinstance(g, int):
                        pe.wait_ge(hl_ready, g * K + (K - 3 + m))
                    both = arw[:, k, :, :].rearrange("p s n -> p (s n)")
                    pe.matmul(arp[m][:, 0:2 * AR], hh[:, k, tok(m)], both, start=(k == 0), stop=False)
                    ins = pe.matmul(arp[m][:, 0:2 * AR], hl[:, k, tok(m)], both, start=False,
                                    stop=(k == K - 1))
                    if k == K - 1:
                        ins.then_inc(ar_done, 1)

            for k in range(3):
                transpose_h(0, k)
            for k in range(K):
                ar_slice(0, k)
                if k == 0:
                    pe.wait_ge(bank_read, M * ITS)
                if k + 3 < K:
                    transpose_h(0, k + 3)

            def group(g, last):
                for j in range(NB):
                    def w_product(m, kk):
                        k, part = WK * q + kk, slice(kk * NW, (kk + 1) * NW)
                        if k == 0 and j > 0 and m > 0:
                            pe.wait_ge(out_ready, g * ITS + (M * (j - 1) + m + 1))
                        elif k == 0 and j > 1:
                            pe.wait_ge(out_ready, g * ITS + (M * (j - 2) + 1))
                        return three(bank(j, m)[:, :], hh[:, k, tok(m)], hl[:, k, tok(m)],
                                     wh[s][:, part], wl[s][:, part], k == 0, False)

                    for q in range(WP):
                        X = WP * j + q
                        s = X % RING
                        pe.wait_ge(wl_ready, g * WG + (LEAD + X + 1))
                        if q < WP - 1:
                            for kk in range(WK):
                                for m in range(M):
                                    ins = w_product(m, kk)
                                if kk == WK - 1:
                                    ins.then_inc(w_used, 1)
                                if j == NB - 1 and not last:
                                    transpose_h(g + 1, WK * q + kk)
                            if j == 0 and q == 3:
                                pe.wait_ge(mids_ready, g + 1)
                                for m in range(M):
                                    ins = pe.transpose(colp[:, tok(m)],
                                                       mids[:, m, :, :].rearrange("p e r -> p (e r)"),
                                                       idf[:, :])
                                ins.then_inc(mt_ready, 1)
                        else:
                            if j == 0:
                                pe.wait_ge(mtl_ready, g + 1)
                            for m in range(M):
                                for kk in range(WK):
                                    ins = w_product(m, kk)
                                if m == M - 1:
                                    ins.then_inc(w_used, 1)
                                    if j == NB - 1 and not last:
                                        transpose_h(g + 1, K - 2)
                                        transpose_h(g + 1, K - 1)
                                cols = slice(j * NW, (j + 1) * NW)
                                three(bank(j, m)[:, :], mth[:, tok(m)], mtl[:, tok(m)],
                                      bh[:, cols], bl[:, cols], False, True).then_inc(acc_done, 1)
                if not last:
                    for k in range(K):
                        ar_slice(g + 1, k)
                        if k == 0:
                            pe.wait_ge(out_ready, g * ITS + ITS)

            with pe.Fori(0, G - 1) as g:
                group(g, False)
            group(G - 1, True)


def kernel(x, ctx_4096, g_xattn, g_ffn, L0_xattn_x1_scale, L0_xattn_x1_zp, L0_xattn_x2_scale,
           L0_xattn_x2_zp, L0_ffn_base_W, L0_ffn_router_W, L0_ffn_lora_A, L0_ffn_lora_B):
    import numpy as np
    import concourse.bacc as bacc
    from concourse.bass_utils import run_bass_kernel_spmd

    scal = [L0_xattn_x1_scale, L0_xattn_x1_zp, L0_xattn_x2_scale, L0_xattn_x2_zp, g_xattn, g_ffn]
    lora_a = np.transpose(np.asarray(L0_ffn_lora_A), (1, 0, 2)).reshape(D, ER)
    arrays = {
        "in_x": np.asarray(x).reshape(TOK, D),
        "in_ctx": np.asarray(ctx_4096),
        "in_wt": np.asarray(L0_ffn_base_W).T,
        "in_ar": np.concatenate([lora_a, np.asarray(L0_ffn_router_W).T], axis=1),
        "in_lb": np.asarray(L0_ffn_lora_B).reshape(ER, D),
        "in_scal": np.broadcast_to(np.concatenate([np.asarray(s).reshape(1) for s in scal])[None, :], (P, 6)),
    }
    arrays = {n: np.ascontiguousarray(a) for n, a in arrays.items()}
    nc = bacc.Bacc("TRN2", target_bir_lowering=False, num_devices=1, dynamic_dma_scratch_size=4096)
    args = [nc.dram_tensor(n, a.shape, F32, kind="ExternalInput").ap() for n, a in arrays.items()]
    args.append(nc.dram_tensor("x1_scratch", (TOK, D), F32, kind="Internal").ap())
    args.append(nc.dram_tensor("out_0", (TOK, D), F32, kind="ExternalOutput").ap())
    build(nc, *args)
    r = run_bass_kernel_spmd(nc, [arrays], core_ids=[0])
    return r.results[0]["out_0"].reshape(np.asarray(x).shape)
```
